# Optimizing a Trainium2 kernel written in Bass

```python
import numpy as np
import jax
import jax.numpy as jnp

def _softmax(x, axis=-1):
    return jax.nn.softmax(x, axis=axis)

def _gelu(x):
    return jax.nn.gelu(x, approximate=True)

def _silu(x):
    return jax.nn.silu(x)

def _sigmoid(x):
    return jax.nn.sigmoid(x)

def _layernorm(x, axis=-1, eps=1e-05):
    m = jnp.mean(x, axis=axis, keepdims=True)
    v = jnp.var(x, axis=axis, keepdims=True)
    return (x - m) / jnp.sqrt(v + eps)

def _scatter_add(tgt, idx, src, axis=0):
    return tgt.at[idx].add(src)

def _segment_sum(src, seg, n):
    return jax.ops.segment_sum(src, seg, n)
kernel_name = 'mk_decoder_preln_d1_seqx_r4_7481f9'

def setup_inputs(seed: int=0):
    np.random.seed(seed)
    _w = jnp.asarray

    def _rec_inputs():
        import jax
        import jax.numpy as jnp
        _rk = jax.random.key(seed)
        x = -0.0002928 + 1 * jax.random.normal(jax.random.fold_in(_rk, 1), (64, 256, 256), jnp.float32)
        _lenS = 256 - jax.random.randint(jax.random.fold_in(_rk, 7), (64,), 0, max(1, 256 // 4) + 1, jnp.int32)
        _lenS2 = 120 - jax.random.randint(jax.random.fold_in(_rk, 8), (64,), 0, max(1, 120 // 4) + 1, jnp.int32)
        _ctx_1024P = jax.random.normal(jax.random.fold_in(_rk, 11), (64, 16, 256), jnp.float32)
        _ctx_1024c = jax.random.dirichlet(jax.random.fold_in(_rk, 511), 0.3 * jnp.ones((16,), jnp.float32), (64, 120))
        _ctx_1024t = jnp.einsum('bsk,bkd->bsd', _ctx_1024c, _ctx_1024P)
        _ctx_1024t = _ctx_1024t * jax.lax.rsqrt(jnp.mean(jnp.square(_ctx_1024t)) + 1e-12) * 0.953939
        ctx_1024 = -1.39393e-06 + 0.999914 * (_ctx_1024t + 0.3 * jax.random.normal(jax.random.fold_in(_rk, 611), (64, 120, 256), jnp.float32))
        return (x, ctx_1024)
    x, ctx_1024 = _rec_inputs()

    def _L0_attn_setup():
        import math
        import jax, jax.numpy as jnp
        import numpy as np
        HIDDEN = 256
        HEADS = 16
        HEAD_DIM = HIDDEN // HEADS
        KERNEL = 7
        DILATION = 1
        SCALE = 1.0 / math.sqrt(HEAD_DIM)
        BATCH, SEQ = (2, 512)

        def neighborhood_mask(seq_len: int) -> jnp.ndarray:
            half = KERNEL // 2
            i = jnp.arange(seq_len)[:, None]
            j = jnp.arange(seq_len)[None, :]
            d = j - i
            return (jnp.abs(d) <= half * DILATION) & (d % DILATION == 0)
        key = jax.random.key(seed)
        ks = jax.random.split(key, 9)
        s = 0.02
        return {'hidden_states': jax.random.normal(ks[0], (BATCH, SEQ, HIDDEN), jnp.float32), 'Wq': jax.random.normal(ks[1], (HIDDEN, HIDDEN), jnp.float32) * s, 'bq': jnp.zeros((HIDDEN,), jnp.float32), 'Wk': jax.random.normal(ks[2], (HIDDEN, HIDDEN), jnp.float32) * s, 'bk': jnp.zeros((HIDDEN,), jnp.float32), 'Wv': jax.random.normal(ks[3], (HIDDEN, HIDDEN), jnp.float32) * s, 'bv': jnp.zeros((HIDDEN,), jnp.float32), 'Wo': jax.random.normal(ks[4], (HIDDEN, HIDDEN), jnp.float32) * s, 'bo': jnp.zeros((HIDDEN,), jnp.float32)}
    _L0_attn_all = _L0_attn_setup()
    _L0_attn_in = {k: v for k, v in _L0_attn_all.items() if k in ('Wq', 'bq', 'Wk', 'bk', 'Wv', 'bv', 'Wo', 'bo')}
    del _L0_attn_all

    def _L0_xattn_setup():
        import jax, jax.numpy as jnp
        import numpy as np
        DIM = 256
        NUM_HEADS = 16
        HEAD_DIM = DIM // NUM_HEADS
        SCALE = HEAD_DIM ** (-0.5)
        key = jax.random.key(seed)
        ks = jax.random.split(key, 11)
        B, SQ, SKV = (2, 512, 512)
        s = DIM ** (-0.5)
        return {'q': jax.random.normal(ks[0], (B, SQ, DIM), jnp.float32), 'k': jax.random.normal(ks[1], (B, SKV, DIM), jnp.float32), 'v': jax.random.normal(ks[2], (B, SKV, DIM), jnp.float32), 'Wq': jax.random.normal(ks[3], (DIM, DIM), jnp.float32) * s, 'bq': jnp.zeros((DIM,), jnp.float32), 'Wk': jax.random.normal(ks[4], (DIM, DIM), jnp.float32) * s, 'bk': jnp.zeros((DIM,), jnp.float32), 'Wv': jax.random.normal(ks[5], (DIM, DIM), jnp.float32) * s, 'bv': jnp.zeros((DIM,), jnp.float32), 'Wo': jax.random.normal(ks[6], (DIM, DIM), jnp.float32) * s, 'bo': jnp.zeros((DIM,), jnp.float32)}
    _L0_xattn_all = _L0_xattn_setup()
    _L0_xattn_in = {k: v for k, v in _L0_xattn_all.items() if k in ('Wq', 'bq', 'Wk', 'bk', 'Wv', 'bv', 'Wo', 'bo')}
    del _L0_xattn_all

    def _L0_ffn_setup():
        import jax, jax.numpy as jnp
        import numpy as np
        D, H, NE, K, ED = (256, 16, 8, 2, 1024)
        B, S = (4, 256)
        EPS = 1e-06

        def rmsnorm(x, w):
            ms = jnp.mean(jnp.square(x.astype(jnp.float32)), axis=-1, keepdims=True)
            return x * jax.lax.rsqrt(ms + EPS).astype(x.dtype) * w

        def attn(x, qkv_w, o_w):
            b, s, d = x.shape
            hd = d // H
            qkv = (x @ qkv_w.T).reshape(b, s, 3, H, hd).transpose(2, 0, 3, 1, 4)
            q, k, v = (qkv[0], qkv[1], qkv[2])
            a = jnp.einsum('bhqd,bhkd->bhqk', q, k) * hd ** (-0.5)
            mask = jnp.triu(jnp.ones((s, s), dtype=bool), 1)
            a = jax.nn.softmax(jnp.where(mask, -1000000000.0, a), axis=-1)
            out = jnp.einsum('bhqk,bhkd->bhqd', a, v).transpose(0, 2, 1, 3).reshape(b, s, d)
            return out @ o_w.T

        def moe(x, gate_w, up_w, down_w):
            b, s, d = x.shape
            xf = x.reshape(b * s, d)
            gp = jax.nn.softmax(xf @ gate_w.T, axis=-1)
            ew, _ = jax.lax.top_k(gp, K)
            ew = ew / (jnp.sum(ew, axis=-1, keepdims=True) + 1e-09)
            ef = jax.nn.silu(xf @ up_w.T) @ down_w.T
            out = ef * jnp.sum(ew, axis=-1, keepdims=True)
            return out.reshape(b, s, d)
        key = jax.random.key(seed)
        ks = jax.random.split(key, 8)
        sd = 1.0 / np.sqrt(D)
        se = 1.0 / np.sqrt(ED)
        return {'x': jax.random.normal(ks[0], (B, S, D), dtype=jnp.float32), 'n1_w': jnp.ones((D,), jnp.float32), 'qkv_w': jax.random.normal(ks[1], (3 * D, D), jnp.float32) * sd, 'o_w': jax.random.normal(ks[2], (D, D), jnp.float32) * sd, 'n2_w': jnp.ones((D,), jnp.float32), 'gate_w': jax.random.normal(ks[3], (NE, D), jnp.float32) * sd, 'up_w': jax.random.normal(ks[4], (ED, D), jnp.float32) * sd, 'down_w': jax.random.normal(ks[5], (D, ED), jnp.float32) * se}
    _L0_ffn_all = _L0_ffn_setup()
    _L0_ffn_in = {k: v for k, v in _L0_ffn_all.items() if k in ('n1_w', 'qkv_w', 'o_w', 'n2_w', 'gate_w', 'up_w', 'down_w')}
    del _L0_ffn_all
    return {'x': x, 'ctx_1024': ctx_1024, 'L0_attn_Wq': _L0_attn_in['Wq'], 'L0_attn_bq': _L0_attn_in['bq'], 'L0_attn_Wk': _L0_attn_in['Wk'], 'L0_attn_bk': _L0_attn_in['bk'], 'L0_attn_Wv': _L0_attn_in['Wv'], 'L0_attn_bv': _L0_attn_in['bv'], 'L0_attn_Wo': _L0_attn_in['Wo'], 'L0_attn_bo': _L0_attn_in['bo'], 'L0_xattn_Wq': _L0_xattn_in['Wq'], 'L0_xattn_bq': _L0_xattn_in['bq'], 'L0_xattn_Wk': _L0_xattn_in['Wk'], 'L0_xattn_bk': _L0_xattn_in['bk'], 'L0_xattn_Wv': _L0_xattn_in['Wv'], 'L0_xattn_bv': _L0_xattn_in['bv'], 'L0_xattn_Wo': _L0_xattn_in['Wo'], 'L0_xattn_bo': _L0_xattn_in['bo'], 'L0_ffn_n1_w': _L0_ffn_in['n1_w'], 'L0_ffn_qkv_w': _L0_ffn_in['qkv_w'], 'L0_ffn_o_w': _L0_ffn_in['o_w'], 'L0_ffn_n2_w': _L0_ffn_in['n2_w'], 'L0_ffn_gate_w': _L0_ffn_in['gate_w'], 'L0_ffn_up_w': _L0_ffn_in['up_w'], 'L0_ffn_down_w': _L0_ffn_in['down_w']}

def reference(x, ctx_1024, L0_attn_Wq, L0_attn_bq, L0_attn_Wk, L0_attn_bk, L0_attn_Wv, L0_attn_bv, L0_attn_Wo, L0_attn_bo, L0_xattn_Wq, L0_xattn_bq, L0_xattn_Wk, L0_xattn_bk, L0_xattn_Wv, L0_xattn_bv, L0_xattn_Wo, L0_xattn_bo, L0_ffn_n1_w, L0_ffn_qkv_w, L0_ffn_o_w, L0_ffn_n2_w, L0_ffn_gate_w, L0_ffn_up_w, L0_ffn_down_w):
    import jax
    import jax.numpy as jnp

    def _L0_attn_ref(hidden_states, Wq, bq, Wk, bk, Wv, bv, Wo, bo):
        import math
        import jax, jax.numpy as jnp
        import numpy as np
        HIDDEN = 256
        HEADS = 16
        HEAD_DIM = HIDDEN // HEADS
        KERNEL = 7
        DILATION = 1
        SCALE = 1.0 / math.sqrt(HEAD_DIM)
        BATCH, SEQ = (2, 512)

        def neighborhood_mask(seq_len: int) -> jnp.ndarray:
            half = KERNEL // 2
            i = jnp.arange(seq_len)[:, None]
            j = jnp.arange(seq_len)[None, :]
            d = j - i
            return (jnp.abs(d) <= half * DILATION) & (d % DILATION == 0)
        B, S, H = hidden_states.shape
        q = hidden_states @ Wq.T + bq
        k = hidden_states @ Wk.T + bk
        v = hidden_states @ Wv.T + bv
        q = q.reshape(B, S, HEADS, HEAD_DIM).transpose(0, 2, 1, 3)
        k = k.reshape(B, S, HEADS, HEAD_DIM).transpose(0, 2, 1, 3)
        v = v.reshape(B, S, HEADS, HEAD_DIM).transpose(0, 2, 1, 3)
        scores = jnp.einsum('bhqd,bhkd->bhqk', q, k) * SCALE
        mask = neighborhood_mask(S)
        scores = jnp.where(mask[None, None], scores, -jnp.inf)
        attn = jax.nn.softmax(scores, axis=-1)
        out = jnp.einsum('bhqk,bhkd->bhqd', attn, v)
        out = out.transpose(0, 2, 1, 3).reshape(B, S, H)
        return out @ Wo.T + bo

    def _L0_xattn_ref(q, k, v, Wq, bq, Wk, bk, Wv, bv, Wo, bo):
        import jax, jax.numpy as jnp
        import numpy as np
        DIM = 256
        NUM_HEADS = 16
        HEAD_DIM = DIM // NUM_HEADS
        SCALE = HEAD_DIM ** (-0.5)
        B, SQ, _ = q.shape
        SKV = k.shape[1]
        qh = (q @ Wq.T + bq).reshape(B, SQ, NUM_HEADS, HEAD_DIM).transpose(0, 2, 1, 3)
        kh = (k @ Wk.T + bk).reshape(B, SKV, NUM_HEADS, HEAD_DIM).transpose(0, 2, 1, 3)
        vh = (v @ Wv.T + bv).reshape(B, SKV, NUM_HEADS, HEAD_DIM).transpose(0, 2, 1, 3)
        attn = jax.nn.softmax(jnp.einsum('bhqd,bhkd->bhqk', qh, kh) * SCALE, axis=-1)
        out = jnp.einsum('bhqk,bhkd->bhqd', attn, vh)
        out = out.transpose(0, 2, 1, 3).reshape(B, SQ, DIM)
        return out @ Wo.T + bo

    def _L0_ffn_ref(x, n1_w, qkv_w, o_w, n2_w, gate_w, up_w, down_w):
        import jax, jax.numpy as jnp
        import numpy as np
        D, H, NE, K, ED = (256, 16, 8, 2, 1024)
        B, S = (4, 256)
        EPS = 1e-06

        def rmsnorm(x, w):
            ms = jnp.mean(jnp.square(x.astype(jnp.float32)), axis=-1, keepdims=True)
            return x * jax.lax.rsqrt(ms + EPS).astype(x.dtype) * w

        def attn(x, qkv_w, o_w):
            b, s, d = x.shape
            hd = d // H
            qkv = (x @ qkv_w.T).reshape(b, s, 3, H, hd).transpose(2, 0, 3, 1, 4)
            q, k, v = (qkv[0], qkv[1], qkv[2])
            a = jnp.einsum('bhqd,bhkd->bhqk', q, k) * hd ** (-0.5)
            mask = jnp.triu(jnp.ones((s, s), dtype=bool), 1)
            a = jax.nn.softmax(jnp.where(mask, -1000000000.0, a), axis=-1)
            out = jnp.einsum('bhqk,bhkd->bhqd', a, v).transpose(0, 2, 1, 3).reshape(b, s, d)
            return out @ o_w.T

        def moe(x, gate_w, up_w, down_w):
            b, s, d = x.shape
            xf = x.reshape(b * s, d)
            gp = jax.nn.softmax(xf @ gate_w.T, axis=-1)
            ew, _ = jax.lax.top_k(gp, K)
            ew = ew / (jnp.sum(ew, axis=-1, keepdims=True) + 1e-09)
            ef = jax.nn.silu(xf @ up_w.T) @ down_w.T
            out = ef * jnp.sum(ew, axis=-1, keepdims=True)
            return out.reshape(b, s, d)
        x = x + attn(rmsnorm(x, n1_w), qkv_w, o_w)
        x = x + moe(rmsnorm(x, n2_w), gate_w, up_w, down_w)
        return x
    x = x + _L0_attn_ref(_layernorm(x, axis=-1), L0_attn_Wq, L0_attn_bq, L0_attn_Wk, L0_attn_bk, L0_attn_Wv, L0_attn_bv, L0_attn_Wo, L0_attn_bo)
    x = x + _L0_xattn_ref(_layernorm(x, axis=-1), ctx_1024, ctx_1024, L0_xattn_Wq, L0_xattn_bq, L0_xattn_Wk, L0_xattn_bk, L0_xattn_Wv, L0_xattn_bv, L0_xattn_Wo, L0_xattn_bo)
    x = x + _L0_ffn_ref(_layernorm(x, axis=-1), L0_ffn_n1_w, L0_ffn_qkv_w, L0_ffn_o_w, L0_ffn_n2_w, L0_ffn_gate_w, L0_ffn_up_w, L0_ffn_down_w)
    return x

_drawn_inputs = setup_inputs


def setup_inputs(seed=0):
    import zlib

    import numpy as np

    out = dict(_drawn_inputs(seed))
    spreads = {'L0_attn_bq': (0.0, 0.8),
     'L0_attn_bk': (0.0, 0.8),
     'L0_attn_bv': (0.0, 0.269),
     'L0_attn_bo': (0.0, 0.1),
     'L0_xattn_bq': (0.0, 0.353),
     'L0_xattn_bk': (0.0, 0.8),
     'L0_xattn_bv': (0.0, 0.1),
     'L0_xattn_bo': (0.0, 0.1),
     'L0_ffn_n1_w': (1.0, 0.2),
     'L0_ffn_n2_w': (1.0, 0.2)}
    factors = {'L0_attn_Wq': 8.0, 'L0_attn_Wk': 8.0, 'L0_ffn_gate_w': 8.0}
    for name, (base, spread) in spreads.items():
        noise = np.random.default_rng([zlib.crc32(name.encode()), seed]).standard_normal(out[name].shape)
        drawn = base * np.exp(spread * noise) if base else spread * noise
        out[name] = jnp.asarray(drawn.astype(out[name].dtype))
    for name, factor in factors.items():
        out[name] = (out[name] * factor).astype(out[name].dtype)
    return out
```

```python
from contextlib import ExitStack

import numpy as np
import concourse.bass as bass
from concourse import mybir

P = 128
STREAMS = 2
HD = 16
GROUPS = 6
QPARTS = (0, 0, 0, 1, 1, 2)
KPARTS = (0, 1, 2, 0, 1, 0)
SHIFT = GROUPS * HD
STACK = SHIFT + 2
HALO = 3
SLOT = 32
NEG = -1e30
LN_EPS = 1e-5
RMS_EPS = 1e-6
SINGLES = 4

ALU = mybir.AluOpType
ACT = mybir.ActivationFunctionType
BF16 = mybir.dt.bfloat16
F32 = mybir.dt.float32
AX_X = mybir.AxisListType.X

LOCAL, CROSS, CAUSAL = 0, 1, 2
WEIGHTS = ("local_q", "local_k", "local_v", "local_o", "cross_q", "cross_k", "cross_v", "cross_o",
           "causal_q", "causal_k", "causal_v", "causal_o")
NAMES = ("local", "cross", "causal")


def max_fills(layer, T, C):
    if layer == LOCAL:
        return [(tb, h, min(3, 16 - h), (P - HALO) * tb, P + HALO) for tb in range(2) for h in range(0, 16, 3)]
    if layer == CROSS:
        return [(tb, h, 4, 0, C) for tb in range(2) for h in range(0, 16, 4)]
    return [(0, h, 4, 0, P) for h in range(0, 16, 4)] + [(1, h, 2, 0, T) for h in range(0, 16, 2)]


def key_blocks(layer, T, C):
    if layer == LOCAL:
        return [(0, P, 0, P + HALO), (P, P, P - HALO, P + HALO)]
    if layer == CROSS:
        return [(0, C, 0, T)]
    return [(0, P, 0, T), (P, P, P, P)]


def stream_steps(T, C):
    out = []
    for layer in (LOCAL, CROSS, CAUSAL):
        out += [(0, "norm", (layer,)), (1, "turn", (layer,))]
        if layer == CROSS:
            out.append((1, "turn_ctx", ()))
        out += [(4, "project", (layer, w)) for w in "qk"] + [(0, "split", (layer,))]
        out.append((4, "project", (layer, "v")))
        out += [(1, "max", (layer, n)) for n in range(len(max_fills(layer, T, C)))]
        out.append((0, "shift", (layer,)))
        nkb = len(key_blocks(layer, T, C))
        for g in range(4):
            out += [(1, "scores", (layer, g, kb)) for kb in range(nkb)]
            if g:
                out.append((1, "values", (layer, g - 1)))
        out.append((1, "values", (layer, 3)))
        out += [(1, "untangle", (layer, tb)) for tb in range(2)]
        out += [(1, "turn_out", (layer,)), (4, "project_out", (layer,))]
    out += [(0, "norm", (3,)), (1, "turn", (3,)), (4, "gate", ())]
    out += [(4, "up", (m,)) for m in range(4)]
    out.append((16, "down", ()))
    return out


def plan(T, C, lag):
    lanes = []
    for s in range(STREAMS):
        at, lane = s * lag, []
        for weight, name, args in stream_steps(T, C):
            lane.append((at, s, name, args))
            at += weight + 0.5
        lanes += lane
    order = [(name, s, args) for _, s, name, args in sorted(lanes, key=lambda x: (x[0], x[1]))]
    fills, rings = {}, {"single": [0] * SINGLES, "pair": [0, 0]}
    turn = {"single": 0, "pair": 0}
    for name, s, args in order:
        if name in ("norm", "split"):
            continue
        kind = "pair" if name == "scores" else "single"
        ring = rings[kind]
        b = turn[kind] % len(ring)
        turn[kind] += 1
        fills[(name, s, args)] = (b if kind == "single" else SINGLES + b, ring[b])
        ring[b] += 1
    return order, fills


def decoder(nc, t, out, lag=30):
    B, T, D = t["x"].shape
    C = t["ctx_1024"].shape[1]
    F = t["up"].shape[1]
    E = t["gate"].shape[1]
    H = D // HD
    SCALE = HD ** -0.5
    assert T == 2 * P and D == 2 * P and C <= P and H == 16 and F == 8 * P
    order, fills = plan(T, C, lag)

    with ExitStack() as ctx:
        def sb(name, shape, dt=F32):
            return ctx.enter_context(nc.sbuf_tensor(name, shape, dt))

        def per_stream(name, shape, dt=F32):
            return [sb(f"{name}{s}", shape, dt) for s in range(STREAMS)]

        ps = ctx.enter_context(nc.psum_tensor("ps", [P, 8, 512], F32))

        W = {n: sb(f"w_{n}", [P, 2, D]) for n in WEIGHTS}
        w_up = sb("w_up", [P, 2, F])
        w_down = sb("w_down", [P, F // P, D])
        w_gate = sb("w_gate", [P, 2, E])
        scale1 = sb("scale1", [P, 2])
        scale2 = sb("scale2", [P, 2])
        bias_qk = {(l, w): sb(f"b_{NAMES[l]}_{w}", [P, 2]) for l in (LOCAL, CROSS) for w in "qk"}
        bias_row = {(l, w): sb(f"b_{NAMES[l]}_{w}", [P, D]) for l in (LOCAL, CROSS) for w in "vo"}
        ident = sb("ident", [P, P])
        neg_half = sb("neg_half", [P, 2])
        ident_b = sb("ident_b", [P, P], BF16)
        band_mask = [sb(f"band_mask{tb}", [P, 3, P + HALO], BF16) for tb in range(2)]
        causal_mask = sb("causal_mask", [P, 4, P], BF16)
        causal_mask_t = sb("causal_mask_t", [P, 2, P], BF16)

        x = per_stream("x", [P, 2, D])
        y = per_stream("y", [P, 2, D])
        xn = per_stream("xn", [P, 2, D])
        xT = per_stream("xT", [P, 2, T])
        cx = per_stream("cx", [P, D])
        cT = per_stream("cT", [P, 2, C])
        rest = {w: per_stream(f"rest_{w}", [P, 2, T]) for w in "qk"}
        parts = {w: per_stream(f"parts_{w}", [P, 2, 3, T], BF16) for w in "qk"}
        stack = {w: per_stream(f"stack_{w}", [P, H, T], BF16) for w in "qk"}
        va = per_stream("va", [P, 2, H, SLOT])
        prob = per_stream("prob", [P, H * (T + P)])
        acc = per_stream("acc", [P, 4, T])
        o = per_stream("o", [P, 2, D])
        oT = per_stream("oT", [P, 2, T])
        stats = per_stream("stats", [P, 2, 6])
        mv = per_stream("mv", [P, 2, 2])
        rstd = per_stream("rstd", [P, 2])
        ms = per_stream("ms", [P, 2])
        rrms = per_stream("rrms", [P, 2])
        nmax = per_stream("nmax", [P, 2, H])
        nmax_rest = per_stream("nmax_rest", [P, 2, H])
        nmax_parts = per_stream("nmax_parts", [P, 2, 2 * H], BF16)
        nmaxT = per_stream("nmaxT", [P, T], BF16)
        rsum = per_stream("rsum", [P, 2, H])
        logits = per_stream("logits", [P, 2, E])
        top = per_stream("top", [P, 2, 8])
        ntop = per_stream("ntop", [P, 2])
        expl = per_stream("expl", [P, 2, E])
        expt = per_stream("expt", [P, 2, 2])
        zsum = per_stream("zsum", [P, 2])
        tsum = per_stream("tsum", [P, 2])
        fac = per_stream("fac", [P, 2])
        fac_r = per_stream("fac_r", [P, 2])
        hid = [prob[s][:, 0:(F // P) * T].rearrange("p (m t) -> p m t", t=T) for s in range(STREAMS)]
        tanh = [prob[s][:, (F // P) * T:(F // P + 4) * T].rearrange("p (a m t) -> p a m t", a=2, t=T)
                for s in range(STREAMS)]
        spill = {(s, w): nc.dram_tensor(f"spill_{w}{s}", (P, 2, 3, T), BF16).ap()
                 for s in range(STREAMS) for w in "qk"}

        setup_dma = ctx.enter_context(nc.semaphore("setup_dma"))
        setup_pool = ctx.enter_context(nc.semaphore("setup_pool"))
        setup_dve = ctx.enter_context(nc.semaphore("setup_dve"))
        sems = []

        def sem(name):
            sems.append(ctx.enter_context(nc.semaphore(name)))
            return sems[-1]

        filled = [sem(f"filled{b}") for b in range(SINGLES + 2)]
        emptied = [sem(f"emptied{b}") for b in range(SINGLES + 2)]
        dve_step = sem("dve_step")

        pool_step = sem("pool_step")

        def wait_taken(eng, name, s, *args):
            b, n = fills[(name, s, args)]
            eng.wait_ge(emptied[b], n + 1)

        def per_sem(name):
            return [sem(f"{name}{s}") for s in range(STREAMS)]

        x_loaded, ctx_loaded = per_sem("x_loaded"), per_sem("ctx_loaded")
        xn_ready, hi_ready, rest_ready = per_sem("xn_ready"), per_sem("hi_ready"), per_sem("rest_ready")
        mid_ready, lo_ready = per_sem("mid_ready"), per_sem("lo_ready")
        spilled = {w: per_sem(f"spilled_{w}") for w in "qk"}
        stacked, nmax_ready, shift_ready = per_sem("stacked"), per_sem("nmax_ready"), per_sem("shift_ready")
        mv_ready, rstd_ready = per_sem("mv_ready"), per_sem("rstd_ready")
        biased = per_sem("biased")
        tops_ready, exps_ready = per_sem("tops_ready"), per_sem("exps_ready")
        tanh_ready, stored = per_sem("tanh_ready"), per_sem("stored")

        def cols(L, kb):
            blocks = key_blocks(L, T, C)
            n = blocks[kb][3]
            first = sum(H * b[3] for b in blocks[:kb])
            return first, n

        def prob_of(s, L, g, kb):
            first, n = cols(L, kb)
            a = first + 4 * g * n
            return prob[s][:, a:a + 4 * n].rearrange("p (h q) -> p h q", q=n)

        with nc.Block() as block:
            @block.sync
            def _(sp):
                n = 0
                for name in WEIGHTS:
                    sp.dma_start(W[name][:], t[name].rearrange("(k p) n -> p k n", p=P)).then_inc(setup_dma, 16)
                for dst, name in ((w_up, "up"), (w_down, "down"), (w_gate, "gate")):
                    sp.dma_start(dst[:], t[name].rearrange("(k p) n -> p k n", p=P)).then_inc(setup_dma, 16)
                for dst, name in ((scale1, "n1"), (scale2, "n2")):
                    sp.dma_start(dst[:], t[name]).then_inc(setup_dma, 16)
                for (l, w), dst in bias_qk.items():
                    sp.dma_start(dst[:], t[f"{NAMES[l]}_b{w}"]).then_inc(setup_dma, 16)
                for (l, w), dst in bias_row.items():
                    src = t[f"{NAMES[l]}_b{w}"].rearrange("(a n) -> a n", a=1).broadcast_to([P, D])
                    sp.dma_start(dst[:], src).then_inc(setup_dma, 16)

            @block.gpsimd
            def _(pool):
                nc.gpsimd.memset(ident[:], 0.0).then_inc(setup_pool, 1)
                nc.gpsimd.memset(ident_b[:], 0.0).then_inc(setup_pool, 1)
                nc.gpsimd.memset(causal_mask[:], 0.0).then_inc(setup_pool, 1)
                nc.gpsimd.memset(causal_mask_t[:], 0.0).then_inc(setup_pool, 1)
                for tb in range(2):
                    nc.gpsimd.memset(band_mask[tb][:], 0.0).then_inc(setup_pool, 1)
                pool.wait_ge(setup_pool, 6)
                for dst in (ident, ident_b):
                    nc.gpsimd.affine_select(out=dst[:], in_=dst[:], compare_op=ALU.not_equal, fill=1.0, base=0,
                                            pattern=[[-1, P]], channel_multiplier=1).then_inc(setup_pool, 1)
                nc.gpsimd.affine_select(out=causal_mask[:], in_=causal_mask[:], compare_op=ALU.is_ge, fill=NEG,
                                        base=0, pattern=[[0, 4], [-1, P]], channel_multiplier=1).then_inc(setup_pool, 1)
                nc.gpsimd.affine_select(out=causal_mask_t[:], in_=causal_mask_t[:], compare_op=ALU.is_ge, fill=NEG,
                                        base=0, pattern=[[0, 2], [1, P]], channel_multiplier=-1).then_inc(setup_pool, 1)
                for tb in range(2):
                    off = (P - HALO) * tb - P * tb
                    nc.gpsimd.affine_select(out=band_mask[tb][:], in_=band_mask[tb][:], compare_op=ALU.is_ge, fill=NEG,
                                            base=off + HALO, pattern=[[0, 3], [1, P + HALO]],
                                            channel_multiplier=-1).then_inc(setup_pool, 1)
                pool.wait_ge(setup_pool, 12)
                for tb in range(2):
                    off = (P - HALO) * tb - P * tb
                    nc.gpsimd.affine_select(out=band_mask[tb][:], in_=band_mask[tb][:], compare_op=ALU.is_ge, fill=NEG,
                                            base=HALO - off, pattern=[[0, 3], [-1, P + HALO]],
                                            channel_multiplier=1).then_inc(setup_pool, 1)

            @block.vector
            def _(dve):
                nc.vector.memset(neg_half[:], -0.5)
                for s in range(STREAMS):
                    nc.vector.memset(va[s][:, :, :, HD + 1:SLOT], 0.0)
                    nc.vector.memset(va[s][:, :, :, HD:HD + 1], 1.0)
                    nc.vector.memset(stack["k"][s][SHIFT:P], 1.0)
                dve.wait_ge(setup_dma, 16 * (len(WEIGHTS) + 5 + len(bias_qk) + len(bias_row)))
                for k in range(2):
                    for name in ("causal_q", "causal_k", "causal_v"):
                        nc.vector.tensor_scalar(W[name][:, k], W[name][:, k], scale1[:, k:k + 1], None, ALU.mult)
                    for w in (w_up, w_gate):
                        nc.vector.tensor_scalar(w[:, k], w[:, k], scale2[:, k:k + 1], None, ALU.mult)
                nc.vector.tensor_scalar(w_down[:], w_down[:], 0.5, None, ALU.mult).then_inc(setup_dve, 1)
                dve.wait_ge(setup_dve, 1)

        with nc.Fori(0, B // STREAMS) as it:
            with nc.Block(no_gpsimd_drain=True) as block:
                @block.sync
                def _(sp):
                    for s in range(STREAMS):
                        src = t["x"].rearrange("(n s) (b p) d -> n s p b d", s=STREAMS, p=P)[bass.ds(it, 1), s]
                        sp.dma_start(x[s][:], src.rearrange("a p b d -> (a p) b d")).then_inc(x_loaded[s], 16)
                    for s in range(STREAMS):
                        src = t["ctx_1024"].rearrange("(n s) c d -> n s c d", s=STREAMS)[bass.ds(it, 1), s]
                        sp.dma_start(cx[s][0:C], src.rearrange("a c d -> (a c) d")).then_inc(ctx_loaded[s], 16)
                    for name, s, args in order:
                        if name == "split":
                            L, = args
                            for n, (w, which) in enumerate((("q", QPARTS), ("k", KPARTS))):
                                keys = C if L == CROSS and w == "k" else T
                                sp.wait_ge(lo_ready[s], 2 * L + n + 1)
                                sp.wait_ge(mid_ready[s], 2 * L + n + 1)
                                sp.wait_ge(hi_ready[s], 2 * L + n + 1)
                                sp.dma_start(spill[s, w][:, :, :, 0:keys],
                                             parts[w][s][:, :, :, 0:keys]).then_inc(spilled[w][s], 16)
                            for n, (w, which) in enumerate((("q", QPARTS), ("k", KPARTS))):
                                keys = C if L == CROSS and w == "k" else T
                                sp.wait_ge(spilled[w][s], 16 * (L + 1))
                                for g, part in enumerate(which):
                                    dst = stack[w][s][HD * g:HD * (g + 1), :, 0:keys]
                                    src = spill[s, w][:, :, part, 0:keys].rearrange("(h i) k t -> i k h t", i=HD)
                                    sp.dma_start(dst.rearrange("i (k h) t -> i k h t", k=2),
                                                 src).then_inc(stacked[s], 16)
                        elif name == "shift":
                            L, = args
                            wait_taken(sp, "shift", s, L)
                            for part in range(2):
                                sp.dma_start(stack["q"][s][SHIFT + part:SHIFT + part + 1],
                                             nmaxT[s][H * part:H * (part + 1)]).then_inc(shift_ready[s], 16)
                        elif name == "down":
                            wait_taken(sp, "down", s)
                            dst = out.rearrange("(n s) (b p) d -> n s p b d", s=STREAMS, p=P)[bass.ds(it, 1), s]
                            sp.dma_start(dst.rearrange("a p b d -> (a p) b d"), x[s][:]).then_inc(stored[s], 16)
                    for s in range(STREAMS):
                        sp.wait_ge(stored[s], 16)

                @block.tensor
                def _(pe):
                    def bank(name, s, args):
                        b, n = fills[(name, s, args)]
                        if n:
                            pe.wait_ge(emptied[b], n)
                        return b

                    for name, s, args in order:
                        if name == "turn":
                            i, = args
                            pe.wait_ge(xn_ready[s], i + 1)
                            b = bank(name, s, args)
                            for k in range(2):
                                for tb in range(2):
                                    at = k * T + tb * P
                                    last = nc.tensor.transpose(ps[:, b, at:at + P], xn[s][:, tb, k * P:(k + 1) * P],
                                                               ident[:])
                            last.then_inc(filled[b], 1)
                        elif name == "turn_ctx":
                            pe.wait_ge(ctx_loaded[s], 16)
                            b = bank(name, s, args)
                            for k in range(2):
                                last = nc.tensor.transpose(ps[:, b, k * C:(k + 1) * C], cx[s][0:C, k * P:(k + 1) * P],
                                                           ident[0:C, 0:C])
                            last.then_inc(filled[b], 1)
                        elif name == "project":
                            L, w = args
                            src, n = xT[s], T
                            wait_taken(pe, "turn", s, L)
                            if L == CROSS and w != "q":
                                wait_taken(pe, "turn_ctx", s)
                                src, n = cT[s], C
                            b = bank(name, s, args)
                            wt = W[f"{NAMES[L]}_{w}"]
                            if w in "qk":
                                for m in range(2):
                                    for k in range(2):
                                        last = nc.tensor.matmul(ps[:, b, m * n:(m + 1) * n], wt[:, k, m * P:(m + 1) * P],
                                                                src[:, k, 0:n], start=(k == 0), stop=(k == 1))
                            else:
                                for tb in range((n + P - 1) // P):
                                    rows = min(P, n - tb * P)
                                    for k in range(2):
                                        last = nc.tensor.matmul(ps[0:rows, b, tb * D:(tb + 1) * D],
                                                                src[:, k, tb * P:tb * P + rows], wt[:, k, :],
                                                                start=(k == 0), stop=(k == 1))
                            last.then_inc(filled[b], 1)
                        elif name == "max":
                            L, f = args
                            tb, h0, hs, key0, keys = max_fills(L, T, C)[f]
                            if f == 0:
                                pe.wait_ge(stacked[s], 16 * 2 * GROUPS * (L + 1))
                            b = bank(name, s, args)
                            to = ps[:, b, 0:hs * keys].rearrange("p (h k) -> p h k", k=keys)
                            for j in range(hs):
                                last = nc.tensor.matmul(to[:, j, :],
                                                        stack["q"][s][0:SHIFT, h0 + j, tb * P:(tb + 1) * P],
                                                        stack["k"][s][0:SHIFT, h0 + j, key0:key0 + keys],
                                                        start=(j == 0), stop=(j == hs - 1), skip_group_check=True)
                            if L == LOCAL:
                                last = nc.tensor.matmul(to, ident_b[:], band_mask[tb][:, 0:hs, :], start=False,
                                                        stop=True, skip_group_check=True)
                            elif L == CAUSAL:
                                last = nc.tensor.matmul(to[:, :, tb * P:(tb + 1) * P], ident_b[:],
                                                        causal_mask[:, 0:hs, :], start=False, stop=True,
                                                        skip_group_check=True)
                            last.then_inc(filled[b], 1)
                        elif name == "shift":
                            L, = args
                            pe.wait_ge(nmax_ready[s], L + 1)
                            b = bank(name, s, args)
                            to = ps[:, b, :].bitcast(BF16)
                            for tb in range(2):
                                last = nc.tensor.transpose(to[0:2 * H, tb * P:(tb + 1) * P], nmax_parts[s][:, tb, :],
                                                           ident_b[:])
                            last.then_inc(filled[b], 1)
                        elif name == "scores":
                            L, g, kb = args
                            key0, keys, q0, qs = key_blocks(L, T, C)[kb]
                            if g == 0 and kb == 0:
                                pe.wait_ge(shift_ready[s], 32 * (L + 1))
                            b = bank(name, s, args)
                            first = SINGLES + 2 * (b - SINGLES)
                            for half in range(2):
                                to = ps[0:keys, first + half, 0:2 * qs].rearrange("p (h q) -> p h q", q=qs)
                                for j in range(2):
                                    head = 4 * g + 2 * half + j
                                    last = nc.tensor.matmul(to[:, j, :],
                                                            stack["k"][s][0:STACK, head, key0:key0 + keys],
                                                            stack["q"][s][0:STACK, head, q0:q0 + qs],
                                                            start=(j == 0), stop=(j == 1), skip_group_check=True)
                                if L == LOCAL:
                                    last = nc.tensor.matmul(to, ident_b[:], band_mask[kb][:, 0:2, :], start=False,
                                                            stop=True, skip_group_check=True)
                                elif L == CAUSAL:
                                    last = nc.tensor.matmul(to[:, :, 0:P], ident_b[:], causal_mask_t[:, 0:2, :],
                                                            start=False, stop=True, skip_group_check=True)
                            last.then_inc(filled[b], 1)
                        elif name == "values":
                            L, g = args
                            blocks = key_blocks(L, T, C)
                            nkb = len(blocks)
                            wait_taken(pe, "project", s, L, "v")
                            for kb in range(nkb):
                                wait_taken(pe, "scores", s, L, g, kb)
                            b = bank(name, s, args)
                            for kb, (key0, keys, q0, qs) in enumerate(blocks):
                                pr = prob_of(s, L, g, kb)
                                for j in range(4):
                                    last = nc.tensor.matmul(ps[SLOT * j:SLOT * (j + 1), b, q0:q0 + qs],
                                                            va[s][0:keys, kb, 4 * g + j, :], pr[0:keys, j, :],
                                                            start=(kb == 0), stop=(kb == nkb - 1),
                                                            tile_position=(0, SLOT * j), skip_group_check=True)
                            last.then_inc(filled[b], 1)
                        elif name == "untangle":
                            L, tb = args
                            wait_taken(pe, "values", s, L, 3)
                            b = bank(name, s, args)
                            for g in range(4):
                                last = nc.tensor.transpose(ps[:, b, g * P:(g + 1) * P],
                                                           acc[s][:, g, tb * P:(tb + 1) * P], ident[:])
                            last.then_inc(filled[b], 1)
                        elif name == "turn_out":
                            L, = args
                            wait_taken(pe, "untangle", s, L, 1)
                            b = bank(name, s, args)
                            for k in range(2):
                                for tb in range(2):
                                    at = k * T + tb * P
                                    last = nc.tensor.transpose(ps[:, b, at:at + P], o[s][:, tb, k * P:(k + 1) * P],
                                                               ident[:])
                            last.then_inc(filled[b], 1)
                        elif name == "project_out":
                            L, = args
                            wait_taken(pe, "turn_out", s, L)
                            b = bank(name, s, args)
                            for tb in range(2):
                                for k in range(2):
                                    last = nc.tensor.matmul(ps[:, b, tb * D:(tb + 1) * D],
                                                            oT[s][:, k, tb * P:(tb + 1) * P],
                                                            W[f"{NAMES[L]}_o"][:, k, :], start=(k == 0), stop=(k == 1))
                            last.then_inc(filled[b], 1)
                        elif name == "gate":
                            wait_taken(pe, "turn", s, 3)
                            b = bank(name, s, args)
                            for tb in range(2):
                                for k in range(2):
                                    last = nc.tensor.matmul(ps[:, b, tb * E:(tb + 1) * E],
                                                            xT[s][:, k, tb * P:(tb + 1) * P], w_gate[:, k, :],
                                                            start=(k == 0), stop=(k == 1))
                            last.then_inc(filled[b], 1)
                        elif name == "up":
                            m2, = args
                            wait_taken(pe, "turn", s, 3)
                            b = bank(name, s, args)
                            for m in range(2):
                                for k in range(2):
                                    last = nc.tensor.matmul(ps[:, b, m * T:(m + 1) * T],
                                                            w_up[:, k, (2 * m2 + m) * P:(2 * m2 + m + 1) * P],
                                                            xT[s][:, k, :], start=(k == 0), stop=(k == 1))
                            last.then_inc(filled[b], 1)
                        elif name == "down":
                            wait_taken(pe, "up", s, 3)
                            b = bank(name, s, args)
                            for tb in range(2):
                                for m in range(F // P):
                                    last = nc.tensor.matmul(ps[:, b, tb * D:(tb + 1) * D],
                                                            hid[s][:, m, tb * P:(tb + 1) * P], w_down[:, m, :],
                                                            start=(m == 0), stop=(m == F // P - 1))
                            last.then_inc(filled[b], 1)

                @block.scalar
                def _(act):
                    def bank(name, s, args):
                        b, n = fills[(name, s, args)]
                        act.wait_ge(filled[b], n + 1)
                        return b

                    for name, s, args in order:
                        if name == "turn":
                            b = bank(name, s, args)
                            nc.scalar.copy(xT[s][:].rearrange("p k t -> p (k t)"),
                                           ps[:, b, :]).then_inc(emptied[b], 1)
                        elif name == "turn_ctx":
                            b = bank(name, s, args)
                            nc.scalar.copy(cT[s][:].rearrange("p k t -> p (k t)"),
                                           ps[:, b, 0:2 * C]).then_inc(emptied[b], 1)
                        elif name == "split":
                            L, = args
                            for n, w in enumerate("qk"):
                                keys = C if L == CROSS and w == "k" else T
                                wait_taken(act, "project", s, L, w)
                                nc.scalar.copy(parts[w][s][:, :, 0, 0:keys],
                                               rest[w][s][:, :, 0:keys]).then_inc(hi_ready[s], 1)
                            for n, w in enumerate("qk"):
                                keys = C if L == CROSS and w == "k" else T
                                act.wait_ge(rest_ready[s], 2 * L + n + 1)
                                nc.scalar.copy(parts[w][s][:, :, 1, 0:keys],
                                               rest[w][s][:, :, 0:keys]).then_inc(mid_ready[s], 1)
                        elif name == "scores":
                            L, g, kb = args
                            key0, keys, q0, qs = key_blocks(L, T, C)[kb]
                            b = bank(name, s, args)
                            first = SINGLES + 2 * (b - SINGLES)
                            dst = prob_of(s, L, g, kb).rearrange("p (a h) q -> p a (h q)", a=2)
                            nc.scalar.activation(dst[0:keys], ps[0:keys, first:first + 2, 0:2 * qs], ACT.Exp,
                                                 scale=SCALE).then_inc(emptied[b], 1)
                        elif name == "values":
                            L, g = args
                            b = bank(name, s, args)
                            nc.scalar.copy(acc[s][:, g, :],
                                           ps[:, b, 0:T]).then_inc(emptied[b], 1)
                        elif name == "turn_out":
                            b = bank(name, s, args)
                            nc.scalar.copy(oT[s][:].rearrange("p k t -> p (k t)"),
                                           ps[:, b, :]).then_inc(emptied[b], 1)
                        elif name == "gate":
                            act.wait_ge(tops_ready[s], 1)
                            for tb in range(2):
                                nc.scalar.activation(expl[s][:, tb, :], logits[s][:, tb, :], ACT.Exp,
                                                     bias=ntop[s][:, tb:tb + 1], accum_out=zsum[s][:, tb:tb + 1])
                                last = nc.scalar.activation(expt[s][:, tb, :], top[s][:, tb, 0:2], ACT.Exp,
                                                            bias=ntop[s][:, tb:tb + 1],
                                                            accum_out=tsum[s][:, tb:tb + 1])
                            last.then_inc(exps_ready[s], 1)
                        elif name == "up":
                            m2, = args
                            b = bank(name, s, args)
                            if m2 >= 2:
                                wait_taken(act, "up", s, m2 - 2)
                            nc.scalar.activation(tanh[s][:, m2 % 2].rearrange("p m t -> p (m t)"), ps[:, b, :],
                                                 ACT.Tanh, scale=0.5).then_inc(tanh_ready[s], 1)

                @block.gpsimd
                def _(pool):
                    steps = [0]

                    def settle(ins):
                        steps[0] += 1
                        ins.then_inc(pool_step, 1)
                        pool.wait_ge(pool_step, steps[0])

                    for name, s, args in order:
                        if name == "norm":
                            i, = args
                            pool.wait_ge(mv_ready[s], i + 1)
                            mean, var = mv[s][:, :, 0], mv[s][:, :, 1]
                            if i < 3:
                                settle(nc.gpsimd.tensor_scalar(ms[s][:], var, LN_EPS, None, ALU.add))
                                last = nc.gpsimd.tensor_tensor(rstd[s][:], ms[s][:], neg_half[:], ALU.pow)
                            if i == 2:
                                settle(last)
                                settle(nc.gpsimd.tensor_tensor(ms[s][:], rstd[s][:], rstd[s][:], ALU.mult))
                                settle(nc.gpsimd.tensor_tensor(ms[s][:], ms[s][:], var, ALU.mult))
                            elif i == 3:
                                settle(nc.gpsimd.tensor_tensor(ms[s][:], mean, mean, ALU.mult))
                                settle(nc.gpsimd.tensor_tensor(ms[s][:], ms[s][:], var, ALU.add))
                            if i >= 2:
                                settle(nc.gpsimd.tensor_scalar(ms[s][:], ms[s][:], RMS_EPS, None, ALU.add))
                                last = nc.gpsimd.tensor_tensor(rrms[s][:], ms[s][:], neg_half[:], ALU.pow)
                            last.then_inc(rstd_ready[s], 1)
                            if i < 2:
                                pool.wait_ge(xn_ready[s], i + 1)
                                row = bias_row[i, "o"]
                                for tb in range(2):
                                    last = nc.gpsimd.tensor_tensor(x[s][:, tb, :], x[s][:, tb, :], row[:], ALU.add)
                                last.then_inc(biased[s], 1)
                            elif i == 3:
                                wait_taken(pool, "project_out", s, CAUSAL)
                                nc.gpsimd.tensor_tensor(x[s][:], x[s][:], y[s][:], ALU.add).then_inc(biased[s], 1)

                @block.vector
                def _(dve):
                    steps = [0]

                    def settle(ins):
                        steps[0] += 1
                        ins.then_inc(dve_step, 1)
                        dve.wait_ge(dve_step, steps[0])

                    def bank(name, s, args):
                        b, n = fills[(name, s, args)]
                        dve.wait_ge(filled[b], n + 1)
                        return b

                    for name, s, args in order:
                        if name == "norm":
                            i, = args
                            src = y[s] if i == 3 else x[s]
                            if i == 0:
                                dve.wait_ge(x_loaded[s], 16)
                            else:
                                wait_taken(dve, "project_out", s, i - 1)
                            for tb in range(2):
                                last = nc.vector.bn_stats(stats[s][:, tb, :], src[:, tb, :])
                            settle(last)
                            for tb in range(2):
                                last = nc.vector.bn_aggr(mv[s][:, tb, :], stats[s][:, tb, :])
                            last.then_inc(mv_ready[s], 1)
                            dve.wait_ge(rstd_ready[s], i + 1)
                            if i < 3:
                                dst = xn[s] if i < 2 else y[s]
                                for tb in range(2):
                                    last = nc.vector.tensor_scalar(dst[:, tb, :], src[:, tb, :], mv[s][:, tb, 0:1],
                                                                   rstd[s][:, tb:tb + 1], ALU.subtract, ALU.mult)
                                if i < 2:
                                    last.then_inc(xn_ready[s], 1)
                                else:
                                    settle(last)
                            if i >= 2:
                                for tb in range(2):
                                    last = nc.vector.tensor_scalar(xn[s][:, tb, :], y[s][:, tb, :],
                                                                   rrms[s][:, tb:tb + 1], None, ALU.mult)
                                last.then_inc(xn_ready[s], 1)
                        elif name == "project":
                            L, w = args
                            b = bank(name, s, args)
                            if w in "qk":
                                n = C if L == CROSS and w == "k" else T
                                if L == CAUSAL:
                                    last = nc.vector.tensor_copy(rest[w][s][:].rearrange("p m t -> p (m t)"),
                                                                 ps[:, b, :])
                                else:
                                    for m in range(2):
                                        last = nc.vector.tensor_scalar(rest[w][s][:, m, 0:n],
                                                                       ps[:, b, m * n:(m + 1) * n],
                                                                       bias_qk[L, w][:, m:m + 1], None, ALU.add)
                                last.then_inc(emptied[b], 1)
                            else:
                                blocks = 1 if L == CROSS else 2
                                rows = C if L == CROSS else P
                                for tb in range(blocks):
                                    dst = va[s][0:rows, tb, :, 0:HD]
                                    src = ps[0:rows, b, tb * D:(tb + 1) * D].rearrange("p (h i) -> p h i", i=HD)
                                    if L == CAUSAL:
                                        last = nc.vector.tensor_copy(dst, src)
                                    else:
                                        row = bias_row[L, "v"][0:rows, :].rearrange("p (h i) -> p h i", i=HD)
                                        last = nc.vector.tensor_tensor(dst, src, row, ALU.add)
                                last.then_inc(emptied[b], 1)
                        elif name == "split":
                            L, = args
                            for n, w in enumerate("qk"):
                                keys = C if L == CROSS and w == "k" else T
                                r = rest[w][s][:, :, 0:keys]
                                dve.wait_ge(hi_ready[s], 2 * L + n + 1)
                                nc.vector.tensor_tensor(r, r, parts[w][s][:, :, 0, 0:keys],
                                                        ALU.subtract).then_inc(rest_ready[s], 1)
                            for n, w in enumerate("qk"):
                                keys = C if L == CROSS and w == "k" else T
                                dve.wait_ge(mid_ready[s], 2 * L + n + 1)
                                nc.vector.tensor_tensor(parts[w][s][:, :, 2, 0:keys], rest[w][s][:, :, 0:keys],
                                                        parts[w][s][:, :, 1, 0:keys],
                                                        ALU.subtract).then_inc(lo_ready[s], 1)
                        elif name == "max":
                            L, f = args
                            tb, h0, hs, key0, keys = max_fills(L, T, C)[f]
                            b = bank(name, s, args)
                            nc.vector.tensor_reduce(nmax[s][:, tb, h0:h0 + hs],
                                                    ps[:, b, 0:hs * keys].rearrange("p (h k) -> p h k", k=keys),
                                                    AX_X, ALU.max, negate=True).then_inc(emptied[b], 1)
                        elif name == "shift":
                            L, = args
                            wait_taken(dve, "max", s, L, len(max_fills(L, T, C)) - 1)
                            hi, lo = nmax_parts[s][:, :, 0:H], nmax_parts[s][:, :, H:2 * H]
                            settle(nc.vector.tensor_copy(hi, nmax[s][:]))
                            settle(nc.vector.tensor_tensor(nmax_rest[s][:], nmax[s][:], hi, ALU.subtract))
                            nc.vector.tensor_copy(lo, nmax_rest[s][:]).then_inc(nmax_ready[s], 1)
                            b = bank(name, s, args)
                            nc.vector.tensor_copy(nmaxT[s][0:2 * H, :],
                                                  ps[:, b, :].bitcast(BF16)[0:2 * H, 0:T]).then_inc(emptied[b], 1)
                        elif name == "untangle":
                            L, tb = args
                            b = bank(name, s, args)
                            v = ps[:, b, :].rearrange("p (h i) -> p h i", i=SLOT)
                            settle(nc.vector.reciprocal(rsum[s][:, tb, :], v[:, :, HD]))
                            nc.vector.tensor_tensor(o[s][:, tb, :].rearrange("p (h i) -> p h i", i=HD), v[:, :, 0:HD],
                                                    rsum[s][:, tb, :].unsqueeze(2).to_broadcast([P, H, HD]),
                                                    ALU.mult).then_inc(emptied[b], 1)
                        elif name == "project_out":
                            L, = args
                            b = bank(name, s, args)
                            dst = x[s] if L < 2 else y[s]
                            if L < 2:
                                dve.wait_ge(biased[s], L + 1)
                            v = dst[:].rearrange("p b d -> p (b d)")
                            nc.vector.tensor_tensor(v, v, ps[:, b, :], ALU.add).then_inc(emptied[b], 1)
                        elif name == "gate":
                            b = bank(name, s, args)
                            lg = logits[s]
                            nc.vector.tensor_copy(lg[:].rearrange("p b e -> p (b e)"),
                                                  ps[:, b, 0:2 * E]).then_inc(emptied[b], 1)
                            wait_taken(dve, "gate", s)
                            for tb in range(2):
                                last = nc.vector.max(top[s][:, tb, :], lg[:, tb, :])
                            settle(last)
                            nc.vector.tensor_scalar(ntop[s][:], top[s][:, :, 0], -1.0, None,
                                                    ALU.mult).then_inc(tops_ready[s], 1)
                        elif name == "up":
                            m2, = args
                            b = bank(name, s, args)
                            dve.wait_ge(tanh_ready[s], m2 + 1)
                            nc.vector.scalar_tensor_tensor(
                                hid[s][:, 2 * m2:2 * m2 + 2, :].rearrange("p m t -> p (m t)"),
                                tanh[s][:, m2 % 2].rearrange("p m t -> p (m t)"), 1.0, ps[:, b, :],
                                ALU.add, ALU.mult).then_inc(emptied[b], 1)
                        elif name == "down":
                            dve.wait_ge(exps_ready[s], 1)
                            settle(nc.vector.reciprocal(fac_r[s][:], zsum[s][:]))
                            settle(nc.vector.tensor_tensor(fac[s][:], tsum[s][:], fac_r[s][:], ALU.mult))
                            settle(nc.vector.tensor_scalar(zsum[s][:], fac[s][:], 1e-9, None, ALU.add))
                            settle(nc.vector.reciprocal(fac_r[s][:], zsum[s][:]))
                            settle(nc.vector.tensor_tensor(fac[s][:], fac[s][:], fac_r[s][:], ALU.mult))
                            b = bank(name, s, args)
                            dve.wait_ge(biased[s], 3)
                            for tb in range(2):
                                last = nc.vector.scalar_tensor_tensor(x[s][:, tb, :], ps[:, b, tb * D:(tb + 1) * D],
                                                                      fac[s][:, tb:tb + 1], x[s][:, tb, :],
                                                                      ALU.mult, ALU.add)
                            last.then_inc(emptied[b], 1)

            nc.all_engine_barrier(sems_to_clear=range(sems[0].num, sems[-1].num + 1))


def kernel(**inputs):
    import concourse.bacc as _bacc
    from concourse.bass_utils import run_bass_kernel_spmd as _run

    a = {k: np.asarray(v) for k, v in inputs.items()}
    D = a["x"].shape[-1]
    lay = {"x": a["x"], "ctx_1024": a["ctx_1024"]}
    for name, layer in (("local", "attn"), ("cross", "xattn")):
        for w in "qkvo":
            lay[f"{name}_{w}"] = a[f"L0_{layer}_W{w}"].T
            lay[f"{name}_b{w}"] = a[f"L0_{layer}_b{w}"]
    for n, w in enumerate("qkv"):
        lay[f"causal_{w}"] = a["L0_ffn_qkv_w"][n * D:(n + 1) * D].T
    lay["causal_o"] = a["L0_ffn_o_w"].T
    lay["up"], lay["down"], lay["gate"] = (a[f"L0_ffn_{w}_w"].T for w in ("up", "down", "gate"))
    lay["n1"], lay["n2"] = a["L0_ffn_n1_w"], a["L0_ffn_n2_w"]
    for name in ("local_bq", "local_bk", "cross_bq", "cross_bk", "n1", "n2"):
        lay[name] = lay[name].reshape(2, P).T

    nc = _bacc.Bacc("TRN2", target_bir_lowering=False, num_devices=1)
    arrays, t = {}, {}
    for name, v in lay.items():
        arrays[f"in_{name}"] = np.ascontiguousarray(v)
        t[name] = nc.dram_tensor(f"in_{name}", v.shape, mybir.dt.from_np(v.dtype), kind="ExternalInput").ap()
    out = nc.dram_tensor("out", a["x"].shape, F32, kind="ExternalOutput").ap()
    decoder(nc, t, out)
    r = _run(nc, [arrays], core_ids=[0])
    return r.results[0]["out"]
```

```python
from contextlib import ExitStack

import numpy as np
import concourse.bass as bass
from concourse import mybir

P = 128
STREAMS = 4
HD = 16
GROUPS = 6
RUNS = ((0, 3), (3, 2), (5, 1))
SHIFT = GROUPS * HD
STACK = SHIFT + 2
HALO = 3
SLOT = 32
VW = HD + 1
PROBS = 3
PARTS = 2
NEG = -1e30
LN_EPS = 1e-5
RMS_EPS = 1e-6
SINGLES = 4

ALU = mybir.AluOpType
ACT = mybir.ActivationFunctionType
BF16 = mybir.dt.bfloat16
F32 = mybir.dt.float32
AX_X = mybir.AxisListType.X

LOCAL, CROSS, CAUSAL = 0, 1, 2
WEIGHTS = ("local_q", "local_k", "local_v", "local_o", "cross_q", "cross_k", "cross_v", "cross_o",
           "causal_q", "causal_k", "causal_v", "causal_o")
NAMES = ("local", "cross", "causal")


def max_fills(layer, T, C):
    if layer == LOCAL:
        return [(tb, h, min(3, 16 - h), (P - HALO) * tb, P + HALO) for tb in range(2) for h in range(0, 16, 3)]
    if layer == CROSS:
        return [(tb, h, 4, 0, C) for tb in range(2) for h in range(0, 16, 4)]
    return [(0, h, 4, 0, P) for h in range(0, 16, 4)] + [(1, h, 2, 0, T) for h in range(0, 16, 2)]


def key_blocks(layer, T, C):
    if layer == LOCAL:
        return [(0, P, 0, P + HALO), (P, P, P - HALO, P + HALO)]
    if layer == CROSS:
        return [(0, C, 0, T)]
    return [(0, P, 0, T), (P, P, P, P)]


def stream_steps(T, C):
    out = []

    def step(name, args=(), pe=0.0, then=0.3):
        out.append((name, args, pe, then))

    for layer in (LOCAL, CROSS, CAUSAL):
        step("norm", (layer,), then=3.5)
        step("turn", (layer,), 0.3, 0.6 if layer == CROSS else 1.0)
        if layer == CROSS:
            step("turn_ctx", (), 0.2, 1.0)
        step("project", (layer, "q"), 1.7, 0)
        step("project", (layer, "k"), 0.9 if layer == CROSS else 1.7, 0)
        step("split", (layer, "q"))
        step("project", (layer, "v"), 0.9 if layer == CROSS else 1.7, 0)
        step("split", (layer, "k"), then=3.0)
        step("gather", (layer,), then=7.0)
        fills = len(max_fills(layer, T, C))
        for n in range(fills):
            step("max", (layer, n), 0.3, 1.5 if n == fills - 1 else 0.35)
        step("shift", (layer,), 0.1, 0.5)
        step("shift_in", (layer,), then=2.5)
        nkb = len(key_blocks(layer, T, C))
        for g in range(4):
            for kb in range(nkb):
                step("scores", (layer, g, kb), 0.6, 0.3)
            if g:
                step("values", (layer, g - 1), 0.7, 0.2)
        step("values", (layer, 3), 0.7, 0.5)
        for tb in range(2):
            step("untangle", (layer, tb), 0.3, 0.8 * tb)
        step("turn_out", (layer,), 0.3, 0.8)
        step("project_out", (layer,), 1.7, 0.7)
    step("norm", (3,), then=3.5)
    step("turn", (3,), 0.3, 1.0)
    step("gate", (), 0.9, 0)
    for m in range(4):
        step("up", (m,), 1.7, 0)
    step("down", (), 6.8, 1.0)
    return out


def plan(T, C, lag):
    lanes = [stream_steps(T, C) for _ in range(STREAMS)]
    at, ready, free = [0] * STREAMS, [lag * s for s in range(STREAMS)], 0.0
    order, probs, parts = [], [], []
    open_probs = open_parts = 0
    while any(a < len(lane) for a, lane in zip(at, lanes)):
        best = None
        for s in range(STREAMS):
            if at[s] == len(lanes[s]):
                continue
            name, args, pe, then = lanes[s][at[s]]
            if name == "scores" and args[2] == 0 and open_probs == PROBS:
                continue
            if name == "project" and args[1] == "q" and open_parts == PARTS:
                continue
            start = max(ready[s], free) if pe else ready[s]
            if best is None or start < best[0]:
                best = (start, s)
        start, s = best
        name, args, pe, then = lanes[s][at[s]]
        at[s] += 1
        order.append((name, s, args))
        if pe:
            free = start + pe
        ready[s] = start + pe + then
        if name == "scores" and args[2] == 0:
            probs.append((s, args[0], args[1]))
            open_probs += 1
        elif name == "values":
            open_probs -= 1
        elif name == "project" and args[1] == "q":
            parts.append((s, args[0]))
            open_parts += 1
        elif name == "gather":
            open_parts -= 1
    fills, used, turn = {}, [0] * (SINGLES + 2), [0, 0]
    for name, s, args in order:
        if name in ("norm", "split", "gather", "shift_in"):
            continue
        pair = name == "scores"
        b = SINGLES + turn[1] % 2 if pair else turn[0] % SINGLES
        turn[pair] += 1
        fills[name, s, args] = (b, used[b])
        used[b] += 1
    prob_slot, prob_before, prob_free = {}, {}, [None] * PROBS
    part_slot = {u: n % PARTS for n, u in enumerate(parts)}
    part_before = {u: parts[n - PARTS] if n >= PARTS else None for n, u in enumerate(parts)}
    held = {}
    for name, s, args in order:
        if name == "scores" and args[2] == 0:
            n = next(n for n in range(PROBS) if n not in held.values())
            user = (s, args[0], args[1])
            held[user] = prob_slot[user] = n
            prob_before[user] = prob_free[n]
            prob_free[n] = user
        elif name == "values":
            del held[s, args[0], args[1]]
    seen = set()
    for name, s, args in order:
        if name == "gather":
            seen.add((s, args[0]))
        elif name == "project" and args[1] == "q" and part_before[s, args[0]]:
            assert part_before[s, args[0]] in seen
    return order, fills, prob_slot, prob_before, part_slot, part_before


def decoder(nc, t, out, lag=2.0):
    B, T, D = t["x"].shape
    C = t["ctx_1024"].shape[1]
    F = t["up"].shape[1]
    E = t["gate"].shape[1]
    H = D // HD
    SCALE = HD ** -0.5
    assert T == 2 * P and D == 2 * P and C <= P and H == 16 and F == 8 * P
    order, fills, prob_slot, prob_before, part_slot, part_before = plan(T, C, lag)

    with ExitStack() as ctx:
        def sb(name, shape, dt=F32):
            return ctx.enter_context(nc.sbuf_tensor(name, shape, dt))

        def per_stream(name, shape, dt=F32):
            return [sb(f"{name}{s}", shape, dt) for s in range(STREAMS)]

        ps = ctx.enter_context(nc.psum_tensor("ps", [P, 8, 512], F32))

        W = {n: sb(f"w_{n}", [P, 2, D]) for n in WEIGHTS}
        w_up = sb("w_up", [P, 2, F])
        w_down = sb("w_down", [P, F // P, D])
        w_gate = sb("w_gate", [P, 2, E])
        scale1 = sb("scale1", [P, 2])
        scale2 = sb("scale2", [P, 2])
        bias_qk = {(l, w): sb(f"b_{NAMES[l]}_{w}", [P, 2]) for l in (LOCAL, CROSS) for w in "qk"}
        bias_row = {(l, w): sb(f"b_{NAMES[l]}_{w}", [P, D]) for l in (LOCAL, CROSS) for w in "vo"}
        ident = sb("ident", [P, P])
        neg_half = sb("neg_half", [P, 2])
        ident_b = sb("ident_b", [P, P], BF16)
        band_mask = [sb(f"band_mask{tb}", [P, 3, P + HALO], BF16) for tb in range(2)]
        causal_mask = sb("causal_mask", [P, 4, P], BF16)
        causal_mask_t = sb("causal_mask_t", [P, 2, P], BF16)

        x = per_stream("x", [P, 2, D])
        y = per_stream("y", [P, 2, D])
        cx = [y[s][:, 0, :] for s in range(STREAMS)]
        cT = [y[s][:, 1, 0:2 * C].rearrange("p (k t) -> p k t", k=2) for s in range(STREAMS)]
        xn = per_stream("xn", [P, 2, D])
        o = xn
        xT = per_stream("xT", [P, 2, T])
        rest = per_stream("rest", [P, 2, 2, T])
        acc = [rest[s][:].rearrange("p a b t -> p (a b) t") for s in range(STREAMS)]
        tanh = rest
        hid = per_stream("hid", [P, F // P, T])
        stack_k = per_stream("stack_k", [P, H * T], BF16)
        stack = {"q": [hid[s][:].rearrange("p m t -> p (m t)").bitcast(BF16)
                       for s in range(STREAMS)],
                 "k": [stack_k[s][:] for s in range(STREAMS)]}
        VPAD = H * VW + SLOT - VW
        va = per_stream("va", [P, 2, VPAD])
        va_heads = [va[s][:, :, 0:H * VW].rearrange("p b (h i) -> p b h i", i=VW) for s in range(STREAMS)]
        nmaxT = per_stream("nmaxT", [P, T], BF16)

        parts = {w: [sb(f"parts_{w}_{n}", [P, 3, 2 * T], BF16) for n in range(PARTS)] for w in "qk"}
        prob = [sb(f"prob{n}", [P, 4 * (T + P)]) for n in range(PROBS)]

        stats = per_stream("stats", [P, 2, 6])
        mv = per_stream("mv", [P, 2, 2])
        rstd = per_stream("rstd", [P, 2])
        ms = per_stream("ms", [P, 2])
        rrms = per_stream("rrms", [P, 2])
        nmax = per_stream("nmax", [P, 2, H])
        nmax_rest = per_stream("nmax_rest", [P, 2, H])
        nmax_parts = per_stream("nmax_parts", [P, 2, 2 * H], BF16)
        rsum = per_stream("rsum", [P, 2, H])
        logits = per_stream("logits", [P, 2, E])
        top = per_stream("top", [P, 2, 8])
        ntop = per_stream("ntop", [P, 2])
        expl = per_stream("expl", [P, 2, E])
        expt = per_stream("expt", [P, 2, 2])
        zsum = per_stream("zsum", [P, 2])
        tsum = per_stream("tsum", [P, 2])
        fac = per_stream("fac", [P, 2])
        fac_r = per_stream("fac_r", [P, 2])
        spill = {(s, w): nc.dram_tensor(f"spill_{w}{s}", (3, HD, H // 2, 2 * T), BF16).ap()
                 for s in range(STREAMS) for w in "qk"}

        setup_dma = ctx.enter_context(nc.semaphore("setup_dma"))
        setup_pool = ctx.enter_context(nc.semaphore("setup_pool"))
        setup_dve = ctx.enter_context(nc.semaphore("setup_dve"))
        sems = []

        def sem(name):
            sems.append(ctx.enter_context(nc.semaphore(name)))
            return sems[-1]

        filled = [sem(f"filled{b}") for b in range(SINGLES + 2)]
        emptied = [sem(f"emptied{b}") for b in range(SINGLES + 2)]
        dve_step = sem("dve_step")

        pool_step = sem("pool_step")

        def wait_taken(eng, name, s, *args):
            b, n = fills[(name, s, args)]
            eng.wait_ge(emptied[b], n + 1)

        def per_sem(name):
            return [sem(f"{name}{s}") for s in range(STREAMS)]

        x_loaded, ctx_loaded = per_sem("x_loaded"), per_sem("ctx_loaded")
        xn_ready, hi_ready = per_sem("xn_ready"), per_sem("hi_ready")
        mid_ready = per_sem("mid_ready")
        lo_ready, spilled = ({w: per_sem(f"{n}_{w}") for w in "qk"} for n in ("lo_ready", "spilled"))
        stacked, nmax_ready, shift_ready = per_sem("stacked"), per_sem("nmax_ready"), per_sem("shift_ready")
        mv_ready, rstd_ready = per_sem("mv_ready"), per_sem("rstd_ready")
        biased = per_sem("biased")
        tops_ready, exps_ready = per_sem("tops_ready"), per_sem("exps_ready")
        tanh_ready, stored = per_sem("tanh_ready"), per_sem("stored")

        def part_of(w, s, L, part, n):
            v = parts[w][part_slot[s, L]][:, part if w == "q" else 2 - part, 0:2 * n]
            return v.rearrange("p (k t) -> p k t", t=n)

        def stack_of(w, s, n):
            return stack[w][s][:, 0:H * n].rearrange("p (h t) -> p h t", t=n)

        def prob_of(s, L, g, kb):
            blocks = key_blocks(L, T, C)
            first, n = sum(4 * b[3] for b in blocks[:kb]), blocks[kb][3]
            return prob[prob_slot[s, L, g]][:, first:first + 4 * n].rearrange("p (h q) -> p h q", q=n)

        with nc.Block() as block:
            @block.sync
            def _(sp):
                n = 0
                for name in WEIGHTS:
                    sp.dma_start(W[name][:], t[name].rearrange("(k p) n -> p k n", p=P)).then_inc(setup_dma, 16)
                for dst, name in ((w_up, "up"), (w_down, "down"), (w_gate, "gate")):
                    sp.dma_start(dst[:], t[name].rearrange("(k p) n -> p k n", p=P)).then_inc(setup_dma, 16)
                for dst, name in ((scale1, "n1"), (scale2, "n2")):
                    sp.dma_start(dst[:], t[name]).then_inc(setup_dma, 16)
                for (l, w), dst in bias_qk.items():
                    sp.dma_start(dst[:], t[f"{NAMES[l]}_b{w}"]).then_inc(setup_dma, 16)
                for (l, w), dst in bias_row.items():
                    src = t[f"{NAMES[l]}_b{w}"].rearrange("(a n) -> a n", a=1).broadcast_to([P, D])
                    sp.dma_start(dst[:], src).then_inc(setup_dma, 16)

            @block.gpsimd
            def _(pool):
                nc.gpsimd.memset(ident[:], 0.0).then_inc(setup_pool, 1)
                nc.gpsimd.memset(ident_b[:], 0.0).then_inc(setup_pool, 1)
                nc.gpsimd.memset(causal_mask[:], 0.0).then_inc(setup_pool, 1)
                nc.gpsimd.memset(causal_mask_t[:], 0.0).then_inc(setup_pool, 1)
                for tb in range(2):
                    nc.gpsimd.memset(band_mask[tb][:], 0.0).then_inc(setup_pool, 1)
                pool.wait_ge(setup_pool, 6)
                for dst in (ident, ident_b):
                    nc.gpsimd.affine_select(out=dst[:], in_=dst[:], compare_op=ALU.not_equal, fill=1.0, base=0,
                                            pattern=[[-1, P]], channel_multiplier=1).then_inc(setup_pool, 1)
                nc.gpsimd.affine_select(out=causal_mask[:], in_=causal_mask[:], compare_op=ALU.is_ge, fill=NEG,
                                        base=0, pattern=[[0, 4], [-1, P]], channel_multiplier=1).then_inc(setup_pool, 1)
                nc.gpsimd.affine_select(out=causal_mask_t[:], in_=causal_mask_t[:], compare_op=ALU.is_ge, fill=NEG,
                                        base=0, pattern=[[0, 2], [1, P]], channel_multiplier=-1).then_inc(setup_pool, 1)
                for tb in range(2):
                    off = (P - HALO) * tb - P * tb
                    nc.gpsimd.affine_select(out=band_mask[tb][:], in_=band_mask[tb][:], compare_op=ALU.is_ge, fill=NEG,
                                            base=off + HALO, pattern=[[0, 3], [1, P + HALO]],
                                            channel_multiplier=-1).then_inc(setup_pool, 1)
                pool.wait_ge(setup_pool, 12)
                for tb in range(2):
                    off = (P - HALO) * tb - P * tb
                    nc.gpsimd.affine_select(out=band_mask[tb][:], in_=band_mask[tb][:], compare_op=ALU.is_ge, fill=NEG,
                                            base=HALO - off, pattern=[[0, 3], [-1, P + HALO]],
                                            channel_multiplier=1).then_inc(setup_pool, 1)

            @block.vector
            def _(dve):
                nc.vector.memset(neg_half[:], -0.5)
                for s in range(STREAMS):
                    nc.vector.memset(va[s][:, :, H * VW:VPAD], 0.0)
                    nc.vector.memset(va_heads[s][:, :, :, HD:VW], 1.0)
                    nc.vector.memset(stack["k"][s][SHIFT:P], 1.0)
                dve.wait_ge(setup_dma, 16 * (len(WEIGHTS) + 5 + len(bias_qk) + len(bias_row)))
                for k in range(2):
                    for name in ("causal_q", "causal_k", "causal_v"):
                        nc.vector.tensor_scalar(W[name][:, k], W[name][:, k], scale1[:, k:k + 1], None, ALU.mult)
                    for w in (w_up, w_gate):
                        nc.vector.tensor_scalar(w[:, k], w[:, k], scale2[:, k:k + 1], None, ALU.mult)
                nc.vector.tensor_scalar(w_down[:], w_down[:], 0.5, None, ALU.mult).then_inc(setup_dve, 1)
                dve.wait_ge(setup_dve, 1)

        with nc.Fori(0, B // STREAMS) as it:
            with nc.Block(no_gpsimd_drain=True) as block:
                @block.sync
                def _(sp):
                    for s in range(STREAMS):
                        src = t["x"].rearrange("(n s) (b p) d -> n s p b d", s=STREAMS, p=P)[bass.ds(it, 1), s]
                        sp.dma_start(x[s][:], src.rearrange("a p b d -> (a p) b d")).then_inc(x_loaded[s], 16)
                    for s in range(STREAMS):
                        src = t["ctx_1024"].rearrange("(n s) c d -> n s c d", s=STREAMS)[bass.ds(it, 1), s]
                        sp.dma_start(cx[s][0:C, :], src.rearrange("a c d -> (a c) d")).then_inc(ctx_loaded[s], 16)
                    for name, s, args in order:
                        if name == "split":
                            L, w = args
                            keys = C if L == CROSS and w == "k" else T
                            sp.wait_ge(lo_ready[w][s], L + 1)
                            src = parts[w][part_slot[s, L]][:, :, 0:2 * keys]
                            dst = spill[s, w][:, :, :, 0:2 * keys].rearrange("n i h x -> (i h) n x")
                            sp.dma_start(dst, src).then_inc(spilled[w][s], 16)
                        elif name == "gather":
                            L, = args
                            for w in "qk":
                                keys = C if L == CROSS and w == "k" else T
                                sp.wait_ge(spilled[w][s], 16 * (L + 1))
                                for first, n in RUNS:
                                    part = 0 if w == "q" else 3 - n
                                    src = spill[s, w][part:part + n, :, :, 0:2 * keys].rearrange("n i h x -> (n i) h x")
                                    dst = stack[w][s][HD * first:HD * (first + n), 0:H * keys]
                                    sp.dma_start(dst.rearrange("p (h x) -> p h x", x=2 * keys),
                                                 src).then_inc(stacked[s], 16)
                        elif name == "shift_in":
                            L, = args
                            wait_taken(sp, "shift", s, L)
                            for part in range(2):
                                sp.dma_start(stack_of("q", s, T)[SHIFT + part:SHIFT + part + 1],
                                             nmaxT[s][H * part:H * (part + 1)]).then_inc(shift_ready[s], 16)
                        elif name == "down":
                            wait_taken(sp, "down", s)
                            dst = out.rearrange("(n s) (b p) d -> n s p b d", s=STREAMS, p=P)[bass.ds(it, 1), s]
                            sp.dma_start(dst.rearrange("a p b d -> (a p) b d"), x[s][:]).then_inc(stored[s], 16)
                    for s in range(STREAMS):
                        sp.wait_ge(stored[s], 16)

                @block.tensor
                def _(pe):
                    def bank(name, s, args):
                        b, n = fills[(name, s, args)]
                        if n:
                            pe.wait_ge(emptied[b], n)
                        return b

                    for name, s, args in order:
                        if name == "turn":
                            i, = args
                            pe.wait_ge(xn_ready[s], i + 1)
                            b = bank(name, s, args)
                            for k in range(2):
                                for tb in range(2):
                                    at = k * T + tb * P
                                    last = nc.tensor.transpose(ps[:, b, at:at + P], xn[s][:, tb, k * P:(k + 1) * P],
                                                               ident[:])
                            last.then_inc(filled[b], 1)
                        elif name == "turn_ctx":
                            pe.wait_ge(ctx_loaded[s], 16)
                            b = bank(name, s, args)
                            for k in range(2):
                                last = nc.tensor.transpose(ps[:, b, k * C:(k + 1) * C], cx[s][0:C, k * P:(k + 1) * P],
                                                           ident[0:C, 0:C])
                            last.then_inc(filled[b], 1)
                        elif name == "project":
                            L, w = args
                            src, n = xT[s], T
                            wait_taken(pe, "turn", s, L)
                            if L == CROSS and w != "q":
                                wait_taken(pe, "turn_ctx", s)
                                src, n = cT[s], C
                            b = bank(name, s, args)
                            wt = W[f"{NAMES[L]}_{w}"]
                            if w in "qk":
                                for m in range(2):
                                    for k in range(2):
                                        last = nc.tensor.matmul(ps[:, b, m * n:(m + 1) * n], wt[:, k, m * P:(m + 1) * P],
                                                                src[:, k, 0:n], start=(k == 0), stop=(k == 1))
                            else:
                                for tb in range((n + P - 1) // P):
                                    rows = min(P, n - tb * P)
                                    for k in range(2):
                                        last = nc.tensor.matmul(ps[0:rows, b, tb * D:(tb + 1) * D],
                                                                src[:, k, tb * P:tb * P + rows], wt[:, k, :],
                                                                start=(k == 0), stop=(k == 1))
                            last.then_inc(filled[b], 1)
                        elif name == "max":
                            L, f = args
                            tb, h0, hs, key0, keys = max_fills(L, T, C)[f]
                            if f == 0:
                                pe.wait_ge(stacked[s], 16 * 2 * len(RUNS) * (L + 1))
                            b = bank(name, s, args)
                            to = ps[:, b, 0:hs * keys].rearrange("p (h k) -> p h k", k=keys)
                            qst, kst = stack_of("q", s, T), stack_of("k", s, C if L == CROSS else T)
                            for j in range(hs):
                                last = nc.tensor.matmul(to[:, j, :],
                                                        qst[0:SHIFT, h0 + j, tb * P:(tb + 1) * P],
                                                        kst[0:SHIFT, h0 + j, key0:key0 + keys],
                                                        start=(j == 0), stop=(j == hs - 1), skip_group_check=True)
                            if L == LOCAL:
                                last = nc.tensor.matmul(to, ident_b[:], band_mask[tb][:, 0:hs, :], start=False,
                                                        stop=True, skip_group_check=True)
                            elif L == CAUSAL:
                                last = nc.tensor.matmul(to[:, :, tb * P:(tb + 1) * P], ident_b[:],
                                                        causal_mask[:, 0:hs, :], start=False, stop=True,
                                                        skip_group_check=True)
                            last.then_inc(filled[b], 1)
                        elif name == "shift":
                            L, = args
                            pe.wait_ge(nmax_ready[s], L + 1)
                            b = bank(name, s, args)
                            to = ps[:, b, :].bitcast(BF16)
                            for tb in range(2):
                                last = nc.tensor.transpose(to[0:2 * H, tb * P:(tb + 1) * P], nmax_parts[s][:, tb, :],
                                                           ident_b[:])
                            last.then_inc(filled[b], 1)
                        elif name == "scores":
                            L, g, kb = args
                            key0, keys, q0, qs = key_blocks(L, T, C)[kb]
                            if g == 0 and kb == 0:
                                pe.wait_ge(shift_ready[s], 32 * (L + 1))
                            b = bank(name, s, args)
                            first = SINGLES + 2 * (b - SINGLES)
                            qst, kst = stack_of("q", s, T), stack_of("k", s, C if L == CROSS else T)
                            for half in range(2):
                                to = ps[0:keys, first + half, 0:2 * qs].rearrange("p (h q) -> p h q", q=qs)
                                for j in range(2):
                                    head = 4 * g + 2 * half + j
                                    last = nc.tensor.matmul(to[:, j, :],
                                                            kst[0:STACK, head, key0:key0 + keys],
                                                            qst[0:STACK, head, q0:q0 + qs],
                                                            start=(j == 0), stop=(j == 1), skip_group_check=True)
                                if L == LOCAL:
                                    last = nc.tensor.matmul(to, ident_b[:], band_mask[kb][:, 0:2, :], start=False,
                                                            stop=True, skip_group_check=True)
                                elif L == CAUSAL:
                                    last = nc.tensor.matmul(to[:, :, 0:P], ident_b[:], causal_mask_t[:, 0:2, :],
                                                            start=False, stop=True, skip_group_check=True)
                            last.then_inc(filled[b], 1)
                        elif name == "values":
                            L, g = args
                            blocks = key_blocks(L, T, C)
                            nkb = len(blocks)
                            wait_taken(pe, "project", s, L, "v")
                            for kb in range(nkb):
                                wait_taken(pe, "scores", s, L, g, kb)
                            b = bank(name, s, args)
                            for kb, (key0, keys, q0, qs) in enumerate(blocks):
                                pr = prob_of(s, L, g, kb)
                                for j in range(4):
                                    last = nc.tensor.matmul(ps[SLOT * j:SLOT * (j + 1), b, q0:q0 + qs],
                                                            va[s][0:keys, kb, VW * (4 * g + j):VW * (4 * g + j) + SLOT],
                                                            pr[0:keys, j, :],
                                                            start=(kb == 0), stop=(kb == nkb - 1),
                                                            tile_position=(0, SLOT * j), skip_group_check=True)
                            last.then_inc(filled[b], 1)
                        elif name == "untangle":
                            L, tb = args
                            wait_taken(pe, "values", s, L, 3)
                            b = bank(name, s, args)
                            for g in range(4):
                                last = nc.tensor.transpose(ps[:, b, g * P:(g + 1) * P],
                                                           acc[s][:, g, tb * P:(tb + 1) * P], ident[:])
                            last.then_inc(filled[b], 1)
                        elif name == "turn_out":
                            L, = args
                            wait_taken(pe, "untangle", s, L, 1)
                            b = bank(name, s, args)
                            for k in range(2):
                                for tb in range(2):
                                    at = k * T + tb * P
                                    last = nc.tensor.transpose(ps[:, b, at:at + P], o[s][:, tb, k * P:(k + 1) * P],
                                                               ident[:])
                            last.then_inc(filled[b], 1)
                        elif name == "project_out":
                            L, = args
                            wait_taken(pe, "turn_out", s, L)
                            b = bank(name, s, args)
                            for tb in range(2):
                                for k in range(2):
                                    last = nc.tensor.matmul(ps[:, b, tb * D:(tb + 1) * D],
                                                            xT[s][:, k, tb * P:(tb + 1) * P],
                                                            W[f"{NAMES[L]}_o"][:, k, :], start=(k == 0), stop=(k == 1))
                            last.then_inc(filled[b], 1)
                        elif name == "gate":
                            wait_taken(pe, "turn", s, 3)
                            b = bank(name, s, args)
                            for tb in range(2):
                                for k in range(2):
                                    last = nc.tensor.matmul(ps[:, b, tb * E:(tb + 1) * E],
                                                            xT[s][:, k, tb * P:(tb + 1) * P], w_gate[:, k, :],
                                                            start=(k == 0), stop=(k == 1))
                            last.then_inc(filled[b], 1)
                        elif name == "up":
                            m2, = args
                            wait_taken(pe, "turn", s, 3)
                            b = bank(name, s, args)
                            for m in range(2):
                                for k in range(2):
                                    last = nc.tensor.matmul(ps[:, b, m * T:(m + 1) * T],
                                                            w_up[:, k, (2 * m2 + m) * P:(2 * m2 + m + 1) * P],
                                                            xT[s][:, k, :], start=(k == 0), stop=(k == 1))
                            last.then_inc(filled[b], 1)
                        elif name == "down":
                            wait_taken(pe, "up", s, 3)
                            b = bank(name, s, args)
                            for tb in range(2):
                                for m in range(F // P):
                                    last = nc.tensor.matmul(ps[:, b, tb * D:(tb + 1) * D],
                                                            hid[s][:, m, tb * P:(tb + 1) * P], w_down[:, m, :],
                                                            start=(m == 0), stop=(m == F // P - 1))
                            last.then_inc(filled[b], 1)

                @block.scalar
                def _(act):
                    def bank(name, s, args):
                        b, n = fills[(name, s, args)]
                        act.wait_ge(filled[b], n + 1)
                        return b

                    for name, s, args in order:
                        if name == "turn":
                            b = bank(name, s, args)
                            nc.scalar.copy(xT[s][:].rearrange("p k t -> p (k t)"),
                                           ps[:, b, :]).then_inc(emptied[b], 1)
                        elif name == "turn_ctx":
                            b = bank(name, s, args)
                            nc.scalar.copy(y[s][:, 1, 0:2 * C],
                                           ps[:, b, 0:2 * C]).then_inc(emptied[b], 1)
                        elif name == "project" and args[1] != "v":
                            L, w = args
                            n = C if L == CROSS and w == "k" else T
                            before = part_before[s, L]
                            if before:
                                act.wait_ge(spilled[w][before[0]], 16 * (before[1] + 1))
                            b = bank(name, s, args)
                            hi = part_of(w, s, L, 0, n)
                            v = ps[:, b, 0:2 * n].rearrange("p (m t) -> p m t", t=n)
                            if L == CAUSAL:
                                last = nc.scalar.copy(hi, v)
                            else:
                                for m in range(2):
                                    last = nc.scalar.activation(hi[:, m, :], v[:, m, :], ACT.Identity,
                                                                bias=bias_qk[L, w][:, m:m + 1])
                            last.then_inc(hi_ready[s], 1)
                        elif name == "split":
                            L, w = args
                            n = C if L == CROSS and w == "k" else T
                            wait_taken(act, "project", s, L, w)
                            nc.scalar.copy(part_of(w, s, L, 1, n),
                                           rest[s][:, "qk".index(w), :, 0:n]).then_inc(mid_ready[s], 1)
                        elif name == "scores":
                            L, g, kb = args
                            key0, keys, q0, qs = key_blocks(L, T, C)[kb]
                            b = bank(name, s, args)
                            first = SINGLES + 2 * (b - SINGLES)
                            before = prob_before[s, L, g]
                            if before and kb == 0:
                                b2, n2 = fills["values", before[0], before[1:]]
                                act.wait_ge(filled[b2], n2 + 1)
                            dst = prob_of(s, L, g, kb).rearrange("p (a h) q -> p a (h q)", a=2)
                            nc.scalar.activation(dst[0:keys], ps[0:keys, first:first + 2, 0:2 * qs], ACT.Exp,
                                                 scale=SCALE).then_inc(emptied[b], 1)
                        elif name == "values":
                            L, g = args
                            b = bank(name, s, args)
                            nc.scalar.copy(acc[s][:, g, :],
                                           ps[:, b, 0:T]).then_inc(emptied[b], 1)
                        elif name == "turn_out":
                            b = bank(name, s, args)
                            nc.scalar.copy(xT[s][:].rearrange("p k t -> p (k t)"),
                                           ps[:, b, :]).then_inc(emptied[b], 1)
                        elif name == "gate":
                            act.wait_ge(tops_ready[s], 1)
                            for tb in range(2):
                                nc.scalar.activation(expl[s][:, tb, :], logits[s][:, tb, :], ACT.Exp,
                                                     bias=ntop[s][:, tb:tb + 1], accum_out=zsum[s][:, tb:tb + 1])
                                last = nc.scalar.activation(expt[s][:, tb, :], top[s][:, tb, 0:2], ACT.Exp,
                                                            bias=ntop[s][:, tb:tb + 1],
                                                            accum_out=tsum[s][:, tb:tb + 1])
                            last.then_inc(exps_ready[s], 1)
                        elif name == "up":
                            m2, = args
                            b = bank(name, s, args)
                            if m2 >= 2:
                                wait_taken(act, "up", s, m2 - 2)
                            nc.scalar.activation(tanh[s][:, m2 % 2].rearrange("p m t -> p (m t)"), ps[:, b, :],
                                                 ACT.Tanh, scale=0.5).then_inc(tanh_ready[s], 1)

                @block.gpsimd
                def _(pool):
                    steps = [0]

                    def settle(ins):
                        steps[0] += 1
                        ins.then_inc(pool_step, 1)
                        pool.wait_ge(pool_step, steps[0])

                    for name, s, args in order:
                        if name == "norm":
                            i, = args
                            pool.wait_ge(mv_ready[s], i + 1)
                            mean, var = mv[s][:, :, 0], mv[s][:, :, 1]
                            if i < 3:
                                settle(nc.gpsimd.tensor_scalar(ms[s][:], var, LN_EPS, None, ALU.add))
                                last = nc.gpsimd.tensor_tensor(rstd[s][:], ms[s][:], neg_half[:], ALU.pow)
                            if i == 2:
                                settle(last)
                                settle(nc.gpsimd.tensor_tensor(ms[s][:], rstd[s][:], rstd[s][:], ALU.mult))
                                settle(nc.gpsimd.tensor_tensor(ms[s][:], ms[s][:], var, ALU.mult))
                            elif i == 3:
                                settle(nc.gpsimd.tensor_tensor(ms[s][:], mean, mean, ALU.mult))
                                settle(nc.gpsimd.tensor_tensor(ms[s][:], ms[s][:], var, ALU.add))
                            if i >= 2:
                                settle(nc.gpsimd.tensor_scalar(ms[s][:], ms[s][:], RMS_EPS, None, ALU.add))
                                last = nc.gpsimd.tensor_tensor(rrms[s][:], ms[s][:], neg_half[:], ALU.pow)
                            last.then_inc(rstd_ready[s], 1)
                            if i < 2:
                                pool.wait_ge(xn_ready[s], i + 1)
                                row = bias_row[i, "o"]
                                for tb in range(2):
                                    last = nc.gpsimd.tensor_tensor(x[s][:, tb, :], x[s][:, tb, :], row[:], ALU.add)
                                last.then_inc(biased[s], 1)
                            elif i == 3:
                                wait_taken(pool, "project_out", s, CAUSAL)
                                nc.gpsimd.tensor_tensor(x[s][:], x[s][:], y[s][:], ALU.add).then_inc(biased[s], 1)

                @block.vector
                def _(dve):
                    steps = [0]

                    def settle(ins):
                        steps[0] += 1
                        ins.then_inc(dve_step, 1)
                        dve.wait_ge(dve_step, steps[0])

                    def bank(name, s, args):
                        b, n = fills[(name, s, args)]
                        dve.wait_ge(filled[b], n + 1)
                        return b

                    for name, s, args in order:
                        if name == "norm":
                            i, = args
                            src = y[s] if i == 3 else x[s]
                            if i == 0:
                                dve.wait_ge(x_loaded[s], 16)
                            else:
                                wait_taken(dve, "project_out", s, i - 1)
                            for tb in range(2):
                                last = nc.vector.bn_stats(stats[s][:, tb, :], src[:, tb, :])
                            settle(last)
                            for tb in range(2):
                                last = nc.vector.bn_aggr(mv[s][:, tb, :], stats[s][:, tb, :])
                            last.then_inc(mv_ready[s], 1)
                            dve.wait_ge(rstd_ready[s], i + 1)
                            if i < 3:
                                dst = xn[s] if i < 2 else y[s]
                                for tb in range(2):
                                    last = nc.vector.tensor_scalar(dst[:, tb, :], src[:, tb, :], mv[s][:, tb, 0:1],
                                                                   rstd[s][:, tb:tb + 1], ALU.subtract, ALU.mult)
                                if i < 2:
                                    last.then_inc(xn_ready[s], 1)
                                else:
                                    settle(last)
                            if i >= 2:
                                for tb in range(2):
                                    last = nc.vector.tensor_scalar(xn[s][:, tb, :], y[s][:, tb, :],
                                                                   rrms[s][:, tb:tb + 1], None, ALU.mult)
                                last.then_inc(xn_ready[s], 1)
                        elif name == "project":
                            L, w = args
                            b = bank(name, s, args)
                            if w in "qk":
                                n = C if L == CROSS and w == "k" else T
                                hi = part_of(w, s, L, 0, n)
                                r = rest[s][:, "qk".index(w), :, 0:n]
                                v = ps[:, b, 0:2 * n].rearrange("p (m t) -> p m t", t=n)
                                dve.wait_ge(hi_ready[s], 2 * L + 1 + (w == "k"))
                                if L == CAUSAL:
                                    last = nc.vector.tensor_tensor(r, v, hi, ALU.subtract)
                                else:
                                    for m in range(2):
                                        last = nc.vector.scalar_tensor_tensor(r[:, m, :], v[:, m, :],
                                                                              bias_qk[L, w][:, m:m + 1], hi[:, m, :],
                                                                              ALU.add, ALU.subtract)
                                last.then_inc(emptied[b], 1)
                            else:
                                blocks = 1 if L == CROSS else 2
                                rows = C if L == CROSS else P
                                for tb in range(blocks):
                                    dst = va_heads[s][0:rows, tb, :, 0:HD]
                                    src = ps[0:rows, b, tb * D:(tb + 1) * D].rearrange("p (h i) -> p h i", i=HD)
                                    if L == CAUSAL:
                                        last = nc.vector.tensor_copy(dst, src)
                                    else:
                                        row = bias_row[L, "v"][0:rows, :].rearrange("p (h i) -> p h i", i=HD)
                                        last = nc.vector.tensor_tensor(dst, src, row, ALU.add)
                                last.then_inc(emptied[b], 1)
                        elif name == "split":
                            L, w = args
                            n = C if L == CROSS and w == "k" else T
                            dve.wait_ge(mid_ready[s], 2 * L + 1 + (w == "k"))
                            nc.vector.tensor_tensor(part_of(w, s, L, 2, n), rest[s][:, "qk".index(w), :, 0:n],
                                                    part_of(w, s, L, 1, n),
                                                    ALU.subtract).then_inc(lo_ready[w][s], 1)
                        elif name == "max":
                            L, f = args
                            tb, h0, hs, key0, keys = max_fills(L, T, C)[f]
                            b = bank(name, s, args)
                            nc.vector.tensor_reduce(nmax[s][:, tb, h0:h0 + hs],
                                                    ps[:, b, 0:hs * keys].rearrange("p (h k) -> p h k", k=keys),
                                                    AX_X, ALU.max, negate=True).then_inc(emptied[b], 1)
                        elif name == "shift":
                            L, = args
                            wait_taken(dve, "max", s, L, len(max_fills(L, T, C)) - 1)
                            hi, lo = nmax_parts[s][:, :, 0:H], nmax_parts[s][:, :, H:2 * H]
                            settle(nc.vector.tensor_copy(hi, nmax[s][:]))
                            settle(nc.vector.tensor_tensor(nmax_rest[s][:], nmax[s][:], hi, ALU.subtract))
                            nc.vector.tensor_copy(lo, nmax_rest[s][:]).then_inc(nmax_ready[s], 1)
                            b = bank(name, s, args)
                            nc.vector.tensor_copy(nmaxT[s][0:2 * H, :],
                                                  ps[:, b, :].bitcast(BF16)[0:2 * H, 0:T]).then_inc(emptied[b], 1)
                        elif name == "untangle":
                            L, tb = args
                            b = bank(name, s, args)
                            v = ps[:, b, :].rearrange("p (h i) -> p h i", i=SLOT)
                            settle(nc.vector.reciprocal(rsum[s][:, tb, :], v[:, :, HD]))
                            nc.vector.tensor_tensor(o[s][:, tb, :].rearrange("p (h i) -> p h i", i=HD), v[:, :, 0:HD],
                                                    rsum[s][:, tb, :].unsqueeze(2).to_broadcast([P, H, HD]),
                                                    ALU.mult).then_inc(emptied[b], 1)
                        elif name == "project_out":
                            L, = args
                            b = bank(name, s, args)
                            dst = x[s] if L < 2 else y[s]
                            if L < 2:
                                dve.wait_ge(biased[s], L + 1)
                            v = dst[:].rearrange("p b d -> p (b d)")
                            nc.vector.tensor_tensor(v, v, ps[:, b, :], ALU.add).then_inc(emptied[b], 1)
                        elif name == "gate":
                            b = bank(name, s, args)
                            lg = logits[s]
                            nc.vector.tensor_copy(lg[:].rearrange("p b e -> p (b e)"),
                                                  ps[:, b, 0:2 * E]).then_inc(emptied[b], 1)
                            wait_taken(dve, "gate", s)
                            for tb in range(2):
                                last = nc.vector.max(top[s][:, tb, :], lg[:, tb, :])
                            settle(last)
                            nc.vector.tensor_scalar(ntop[s][:], top[s][:, :, 0], -1.0, None,
                                                    ALU.mult).then_inc(tops_ready[s], 1)
                        elif name == "up":
                            m2, = args
                            b = bank(name, s, args)
                            dve.wait_ge(tanh_ready[s], m2 + 1)
                            nc.vector.scalar_tensor_tensor(
                                hid[s][:, 2 * m2:2 * m2 + 2, :].rearrange("p m t -> p (m t)"),
                                tanh[s][:, m2 % 2].rearrange("p m t -> p (m t)"), 1.0, ps[:, b, :],
                                ALU.add, ALU.mult).then_inc(emptied[b], 1)
                        elif name == "down":
                            dve.wait_ge(exps_ready[s], 1)
                            settle(nc.vector.reciprocal(fac_r[s][:], zsum[s][:]))
                            settle(nc.vector.tensor_tensor(fac[s][:], tsum[s][:], fac_r[s][:], ALU.mult))
                            settle(nc.vector.tensor_scalar(zsum[s][:], fac[s][:], 1e-9, None, ALU.add))
                            settle(nc.vector.reciprocal(fac_r[s][:], zsum[s][:]))
                            settle(nc.vector.tensor_tensor(fac[s][:], fac[s][:], fac_r[s][:], ALU.mult))
                            b = bank(name, s, args)
                            dve.wait_ge(biased[s], 3)
                            for tb in range(2):
                                last = nc.vector.scalar_tensor_tensor(x[s][:, tb, :], ps[:, b, tb * D:(tb + 1) * D],
                                                                      fac[s][:, tb:tb + 1], x[s][:, tb, :],
                                                                      ALU.mult, ALU.add)
                            last.then_inc(emptied[b], 1)

            nc.all_engine_barrier(sems_to_clear=range(sems[0].num, sems[-1].num + 1))


def kernel(**inputs):
    import concourse.bacc as _bacc
    from concourse.bass_utils import run_bass_kernel_spmd as _run

    a = {k: np.asarray(v) for k, v in inputs.items()}
    D = a["x"].shape[-1]
    lay = {"x": a["x"], "ctx_1024": a["ctx_1024"]}
    for name, layer in (("local", "attn"), ("cross", "xattn")):
        for w in "qkvo":
            lay[f"{name}_{w}"] = a[f"L0_{layer}_W{w}"].T
            lay[f"{name}_b{w}"] = a[f"L0_{layer}_b{w}"]
    for n, w in enumerate("qkv"):
        lay[f"causal_{w}"] = a["L0_ffn_qkv_w"][n * D:(n + 1) * D].T
    lay["causal_o"] = a["L0_ffn_o_w"].T
    H = D // HD
    for name in NAMES:
        for w in "qk":
            v = lay[f"{name}_{w}"].reshape(D, H // 2, 2, HD)
            lay[f"{name}_{w}"] = v.transpose(0, 2, 3, 1).reshape(D, D)
    for name in ("local_bq", "local_bk", "cross_bq", "cross_bk"):
        lay[name] = lay[name].reshape(H // 2, 2, HD).transpose(1, 2, 0).reshape(2, P).T
    lay["up"], lay["down"], lay["gate"] = (a[f"L0_ffn_{w}_w"].T for w in ("up", "down", "gate"))
    lay["n1"], lay["n2"] = a["L0_ffn_n1_w"], a["L0_ffn_n2_w"]
    for name in ("n1", "n2"):
        lay[name] = lay[name].reshape(2, P).T

    nc = _bacc.Bacc("TRN2", target_bir_lowering=False, num_devices=1)
    arrays, t = {}, {}
    for name, v in lay.items():
        arrays[f"in_{name}"] = np.ascontiguousarray(v)
        t[name] = nc.dram_tensor(f"in_{name}", v.shape, mybir.dt.from_np(v.dtype), kind="ExternalInput").ap()
    out = nc.dram_tensor("out", a["x"].shape, F32, kind="ExternalOutput").ap()
    decoder(nc, t, out)
    r = _run(nc, [arrays], core_ids=[0])
    return r.results[0]["out"]
```

```python
from contextlib import ExitStack

import numpy as np
import concourse.bass as bass
from concourse import mybir

P = 128
STREAMS = 4
HD = 16
GROUPS = 6
RUNS = ((0, 3), (3, 2), (5, 1))
SHIFT = GROUPS * HD
STACK = SHIFT + 2
HALO = 3
WINDOW = 2 * HALO + 1
HELD = 2 + 2 * HALO
CHUNKS = (tuple(("k", b, j, n) for b in range(2) for j, n in ((0, 3), (3, 2), (5, 2))) +
          tuple(("v", b, h, n) for b in range(2) for h, n in ((0, 6), (6, 5), (11, 5))))
DOTS = 6
SLOT = 32
VW = HD + 1
PROBS = 3
PARTS = 2
NEG = -1e30
ONES_PAIR = float(np.array([0x3F803F80], np.uint32).view(np.float32)[0])
LN_EPS = 1e-5
RMS_EPS = 1e-6
PE_STEPS = ("turn", "turn_ctx", "project_rows", "project", "max", "shift", "scores", "values", "untangle",
            "turn_out", "project_out", "gate", "up", "down")
DMA_SIGNALS = ("x_loaded", "ctx_loaded", "sent_k", "sent_v", "fetched_k", "fetched_v", "spilled_q", "spilled_k",
               "stacked", "shift_ready", "stored")
SINGLES = 4

ALU = mybir.AluOpType
ACT = mybir.ActivationFunctionType
BF16 = mybir.dt.bfloat16
F32 = mybir.dt.float32
AX_X = mybir.AxisListType.X

LOCAL, CROSS, CAUSAL = 0, 1, 2
CUTS = (("moments", (0,)), ("moments", (1,)), ("moments", (2,)), ("moments", (3,)))
LAGS = (19.07, 10.59, 51.08, 91.29)
WEIGHTS = ("local_q", "local_k", "local_v", "local_o", "cross_q", "cross_k", "cross_v", "cross_o",
           "causal_q", "causal_k", "causal_v", "causal_o")
NAMES = ("local", "cross", "causal")


def max_fills(layer, T, C):
    if layer == CROSS:
        return [(tb, h, 4, 0, C) for tb in range(2) for h in range(0, 16, 4)]
    return [(0, h, 4, 0, P) for h in range(0, 16, 4)] + [(1, h, 2, 0, T) for h in range(0, 16, 2)]


def key_blocks(layer, T, C):
    if layer == CROSS:
        return [(0, C, 0, T)]
    return [(0, P, 0, T), (P, P, P, P)]


def stream_steps(T, C):
    out = []

    def step(name, args=(), pe=0.0, then=0.3):
        out.append((name, args, pe, then))

    step("load", then=43.99)
    for layer in (LOCAL, CROSS, CAUSAL):
        step("moments", (layer,), then=(48.67, 34.68, 34.68)[layer])
        step("norm", (layer,), then=(5.39, 2.24, 12.81)[layer])
        step("turn", (layer,), 0.35, 1.26 if layer == CROSS else 2.77)
        if layer == CROSS:
            step("turn_ctx", (), 16.15, 6.58)
        if layer == LOCAL:
            for w in "kvq":
                step("project_rows", (w,), 6.56, 0)
                if w != "q":
                    step("send", (w,), then=3.22)
            for w in "kv":
                step("fetch", (w,), then=8.35)
            for first, end in ((0, DOTS), (DOTS, len(CHUNKS))):
                for c in range(first, end):
                    step("window_times", (c,), then=0.00)
                    if c > first:
                        step("window_reduce", (c - 1,), then=7.80)
                step("window_reduce", (end - 1,), then=1.16)
                if end == DOTS:
                    step("window_max", then=14.79)
                    step("window_exp", then=2.74)
                    step("window_sum", then=0.45)
            step("ones", then=2.69)
        else:
            step("project", (layer, "q"), (0.20, 0.26)[layer - 1], 0)
            step("project", (layer, "k"), 6.88 if layer == CROSS else 7.02, 0)
            step("split", (layer, "q"))
            step("project", (layer, "v"), 1.18 if layer == CROSS else 3.68, 0)
            step("split", (layer, "k"), then=(29.85, 34.88)[layer - 1])
            step("gather", (layer,), then=(31.09, 30.85)[layer - 1])
            fills = len(max_fills(layer, T, C))
            for n in range(fills):
                step("max", (layer, n), 7.39, 0.88 if n == fills - 1 else 2.32)
            step("round_max", (layer,), then=(35.27, 35.27)[layer - 1])
            step("shift", (layer,), (9.56, 10.35)[layer - 1], (8.19, 1.63)[layer - 1])
            step("shift_in", (layer,), then=(18.22, 13.21)[layer - 1])
            nkb = len(key_blocks(layer, T, C))
            for g in range(4):
                for kb in range(nkb):
                    step("scores", (layer, g, kb), (1.81, 2.98)[layer - 1], (1.26, 2.85)[layer - 1])
                if g:
                    step("values", (layer, g - 1), (0.99, 0.77)[layer - 1], (1.08, 0.61)[layer - 1])
            step("values", (layer, 3), (14.64, 1.66)[layer - 1], (15.55, 10.34)[layer - 1])
            for tb in range(2):
                step("untangle", (layer, tb), (3.15, 12.28)[layer - 1], (19.45, 13.69)[layer - 1] * tb)
        step("turn_out", (layer,), (1.81, 2.60, 2.98)[layer], (13.24, 17.00, 8.19)[layer])
        step("project_out", (layer,), (15.59, 15.39, 30.32)[layer], (4.68, 2.65, 2.98)[layer])
    step("moments", (3,), then=11.89)
    step("norm", (3,), then=6.26)
    step("turn", (3,), 3.45, 4.49)
    step("gate", (), 13.90, 0)
    for m in range(4):
        step("up", (m,), 6.58, 0)
    step("weigh", then=20.57)
    step("down", (), 0.44, 37.54)
    step("store", then=0.35)
    return out


def signals(name, args):
    return {"load": {"x_loaded": 16, "ctx_loaded": 16},
            "moments": {"mv_ready": 1, "rstd_ready": 1},
            "norm": {"xn_ready": 1, "biased": 0 if args == (2,) else 1},
            "project": {"hi_ready": 1} if "v" not in args else {},
            "split": {"mid_ready": 1, f"lo_ready_{args[-1]}": 1, f"spilled_{args[-1]}": 16} if args else {},
            "send": {f"sent_{args[0]}": 16} if args else {},
            "fetch": {f"fetched_{args[0]}": 16} if args else {},
            "window_times": {"multiplied": 1},
            "window_reduce": {"reduced": 1},
            "window_sum": {"weighted": 1},
            "window_max": {"centred": 1},
            "window_exp": {"window_exps": 1},
            "ones": {"ones_ready": 1},
            "gather": {"stacked": 16 * 2 * len(RUNS)},
            "round_max": {"nmax_ready": 1},
            "shift_in": {"shift_ready": 32},
            "gate": {"tops_ready": 1, "exps_ready": 1},
            "up": {"tanh_ready": 1},
            "store": {"stored": 16}}.get(name, {})


class Plan:

    def __init__(self, T, C, heads, tails, lags=LAGS):
        lanes = []
        for s in range(STREAMS):
            steps = stream_steps(T, C)
            cut = [step[:2] for step in steps].index(CUTS[s])
            lanes.append(steps[cut:] * tails + steps[:cut] * heads)
        left = [sum(step[2] + step[3] for step in lane) for lane in lanes]
        at, ready, free = [0] * STREAMS, list(lags), 0.0
        self.order = []
        self.prob_slot, self.prob_before, prob_last, prob_open = {}, {}, [None] * PROBS, {}
        self.part_slot, self.part_before, part_last, part_open = {}, {}, [None] * PARTS, {}
        at_scores = set()

        def takes(s):
            name, args, _, _ = lanes[s][at[s]]
            prob = (s, *args[0:2]) if name == "scores" and args[2] == 0 else None
            part = (s, args[0]) if name == "project" and args[1] == "q" else None
            if (name, args) == ("window_times", (0,)):
                part = (s, LOCAL)
            return prob, part

        def may_go(s):
            prob, part = takes(s)
            if prob and (len(prob_open) == PROBS or prob[2] == 0 and len(at_scores) == PROBS - 1):
                return False
            return not (part and len(part_open) == PARTS)

        while any(a < len(lane) for a, lane in zip(at, lanes)):
            start, _, s = min((max(ready[s], free) if lanes[s][at[s]][2] else ready[s], -left[s], s)
                              for s in range(STREAMS) if at[s] < len(lanes[s]) and may_go(s))
            prob, part = takes(s)
            name, args, pe, then = lanes[s][at[s]]
            at[s] += 1
            left[s] -= pe + then
            self.order.append((name, s, args))
            if pe:
                free = start + pe
            ready[s] = start + pe + then
            for user, slots, before, last, is_open in ((prob, self.prob_slot, self.prob_before, prob_last, prob_open),
                                                       (part, self.part_slot, self.part_before, part_last, part_open)):
                if user:
                    n = min((n for n in range(len(last)) if n not in is_open.values()),
                            key=lambda n: max((step for step, slot in enumerate(slots.values()) if slot == n),
                                              default=-1))
                    slots[user] = is_open[user] = n
                    before[user], last[n] = last[n], user
            if name == "scores":
                at_scores.add(s)
            if name == "values":
                del prob_open[s, args[0], args[1]]
                if args[1] == 3:
                    at_scores.remove(s)
            elif name == "gather":
                del part_open[s, args[0]]
            elif (name, args) == ("window_reduce", (len(CHUNKS) - 1,)):
                del part_open[s, LOCAL]
        assert not prob_open and not part_open

        self.place = {step: n for n, step in enumerate(self.order)}
        self.fills, used, turn = {}, [0] * (SINGLES + 2), [0, 0]
        self.reached, self.total = {}, {}
        for name, s, args in self.order:
            for signal, amount in signals(name, args).items():
                self.total[signal, s] = self.total.get((signal, s), 0) + amount
                self.reached[signal, name, s, args] = self.total[signal, s]
            if name not in PE_STEPS:
                continue
            pair = name == "scores"
            b = SINGLES + turn[1] % 2 if pair else turn[0] % SINGLES
            turn[pair] += 1
            self.fills[name, s, args] = (b, used[b])
            used[b] += 1

    def earlier(self, at, step):
        return step in self.place and self.place[step] <= at


def decoder(nc, t, out):
    B, T, D = t["x"].shape
    C = t["ctx_1024"].shape[1]
    F = t["up"].shape[1]
    E = t["gate"].shape[1]
    H = D // HD
    SCALE = HD ** -0.5
    assert T == 2 * P and D == 2 * P and C <= P and H == 16 and F == 8 * P

    with ExitStack() as ctx:
        def sb(name, shape, dt=F32):
            return ctx.enter_context(nc.sbuf_tensor(name, shape, dt))

        def per_stream(name, shape, dt=F32):
            return [sb(f"{name}{s}", shape, dt) for s in range(STREAMS)]

        ps = ctx.enter_context(nc.psum_tensor("ps", [P, 8, 512], F32))

        W = {n: sb(f"w_{n}", [P, 2, D]) for n in WEIGHTS}
        w_up = sb("w_up", [P, 2, F])
        w_down = sb("w_down", [P, F // P, D])
        w_gate = sb("w_gate", [P, 2, E])
        scale1 = sb("scale1", [P, 2])
        scale2 = sb("scale2", [P, 2])
        bias_qk = {(CROSS, w): sb(f"b_{NAMES[CROSS]}_{w}", [P, 2]) for w in "qk"}
        bias_row = {(l, w): sb(f"b_{NAMES[l]}_{w}", [P, D])
                    for l, names in ((LOCAL, "qkvo"), (CROSS, "vo")) for w in names}
        ident = sb("ident", [P, P])
        neg_half = sb("neg_half", [P, 2])
        ident_b = sb("ident_b", [P, P], BF16)
        edge_mask = sb("edge_mask", [P, 2, WINDOW])
        causal_mask = sb("causal_mask", [P, 4, P], BF16)
        causal_mask_t = sb("causal_mask_t", [P, 2, P], BF16)

        x = per_stream("x", [P, 2, D])
        y = per_stream("y", [P, 2, D])
        cx = [y[s][:, 0, :] for s in range(STREAMS)]
        cT = [y[s][:, 1, 0:2 * C].rearrange("p (k t) -> p k t", k=2) for s in range(STREAMS)]
        xn = per_stream("xn", [P, 2, D])
        o = xn
        xT = per_stream("xT", [P, 2, T])
        rest = per_stream("rest", [P, 2, 2, T])
        acc = [rest[s][:].rearrange("p a b t -> p (a b) t") for s in range(STREAMS)]
        tanh = rest
        wide = per_stream("wide", [P, 2 * HELD * D])
        hid = [wide[s][:, 0:F // P * T].rearrange("p (m t) -> p m t", t=T) for s in range(STREAMS)]
        stack = {w: [wide[s][:, n * H * T // 2:(n + 1) * H * T // 2].bitcast(BF16) for s in range(STREAMS)]
                 for n, w in enumerate("qk")}
        token_rows = {"q": [rest[s][:, 0] for s in range(STREAMS)], "k": [rest[s][:, 1] for s in range(STREAMS)],
                      "v": [xn[s][:] for s in range(STREAMS)]}
        window_probs = [xT[s][:].rearrange("p k t -> p (k t)")[:, 0:2 * WINDOW * H]
                        .rearrange("p (b j h) -> p b j h", j=WINDOW, h=H) for s in range(STREAMS)]
        VPAD = H * VW + SLOT - VW
        va = per_stream("va", [P, 2, VPAD])
        va_heads = [va[s][:, :, 0:H * VW].rearrange("p b (h i) -> p b h i", i=VW) for s in range(STREAMS)]
        nmaxT = per_stream("nmaxT", [P, T], BF16)

        parts_qk = [sb(f"parts{n}", [P, 2, 3, 2 * T], BF16) for n in range(PARTS)]
        parts = {w: [parts_qk[n][:, i] for n in range(PARTS)] for i, w in enumerate("qk")}
        prob = [sb(f"prob{n}", [P, 4 * (T + P)]) for n in range(PROBS)]

        stats = per_stream("stats", [P, 2, 6])
        mv = per_stream("mv", [P, 2, 2])
        rstd = per_stream("rstd", [P, 2])
        nmean = per_stream("nmean", [P, 2])
        ms = per_stream("ms", [P, 2])
        rrms = per_stream("rrms", [P, 2])
        nmax = per_stream("nmax", [P, 2, H])
        nmax_rest = per_stream("nmax_rest", [P, 2, H])
        nmax_parts = per_stream("nmax_parts", [P, 2, 2 * H], BF16)
        rsum = per_stream("rsum", [P, 2, H])
        logits = per_stream("logits", [P, 2, E])
        top = per_stream("top", [P, 2, 8])
        ntop = per_stream("ntop", [P, 2])
        expl = per_stream("expl", [P, 2, E])
        expt = per_stream("expt", [P, 2, 2])
        zsum = per_stream("zsum", [P, 2])
        tsum = per_stream("tsum", [P, 2])
        fac = per_stream("fac", [P, 2])
        fac_r = per_stream("fac_r", [P, 2])
        spill = {(s, w): nc.dram_tensor(f"spill_{w}{s}", (3, HD, H // 2, 2 * T), BF16).ap()
                 for s in range(STREAMS) for w in "qk"}

        passed = {(s, w): nc.dram_tensor(f"passed_{w}{s}", (T + 2 * HALO, D), F32).ap()
                  for s in range(STREAMS) for w in "kv"}

        setup_dma = ctx.enter_context(nc.semaphore("setup_dma"))
        setup_zeros = ctx.enter_context(nc.semaphore("setup_zeros"))
        setup_pool = ctx.enter_context(nc.semaphore("setup_pool"))
        setup_dve = ctx.enter_context(nc.semaphore("setup_dve"))
        sems = []

        def sem(name):
            sems.append(ctx.enter_context(nc.semaphore(name)))
            return sems[-1]

        filled = [sem(f"filled{b}") for b in range(SINGLES + 2)]
        emptied = [sem(f"emptied{b}") for b in range(SINGLES + 2)]
        dve_step = sem("dve_step")

        act_step = sem("act_step")
        pool_step = sem("pool_step")

        def per_sem(name):
            return [sem(f"{name}{s}") for s in range(STREAMS)]

        x_loaded, ctx_loaded = per_sem("x_loaded"), per_sem("ctx_loaded")
        xn_ready, hi_ready = per_sem("xn_ready"), per_sem("hi_ready")
        mid_ready = per_sem("mid_ready")
        lo_ready, spilled = ({w: per_sem(f"{n}_{w}") for w in "qk"} for n in ("lo_ready", "spilled"))
        stacked, nmax_ready, shift_ready = per_sem("stacked"), per_sem("nmax_ready"), per_sem("shift_ready")
        mv_ready, rstd_ready = per_sem("mv_ready"), per_sem("rstd_ready")
        biased = per_sem("biased")
        tops_ready, exps_ready = per_sem("tops_ready"), per_sem("exps_ready")
        sent, fetched = ({w: per_sem(f"{n}_{w}") for w in "kv"} for n in ("sent", "fetched"))
        multiplied, reduced, centred = per_sem("multiplied"), per_sem("reduced"), per_sem("centred")
        window_exps, weighted, ones_ready = per_sem("window_exps"), per_sem("weighted"), per_sem("ones_ready")
        tanh_ready, stored = per_sem("tanh_ready"), per_sem("stored")

        def window(w, s, first, *dims):
            held = wide[s][:]
            return bass.AP(held.tensor, held.offset + "kv".index(w) * HELD * D + first, [list(held.ap[0])] +
                           [list(d) for d in dims])

        def chunk_values(c):
            return CHUNKS[c][3] * (D if c < DOTS else HD * WINDOW)

        def stack_of(w, s, n):
            return stack[w][s][:, 0:H * n].rearrange("p (h t) -> p h t", t=n)

        signal_of = {"x_loaded": x_loaded, "ctx_loaded": ctx_loaded, "xn_ready": xn_ready, "hi_ready": hi_ready,
                     "mid_ready": mid_ready, "lo_ready_q": lo_ready["q"], "lo_ready_k": lo_ready["k"],
                     "spilled_q": spilled["q"], "spilled_k": spilled["k"], "stacked": stacked,
                     "nmax_ready": nmax_ready, "shift_ready": shift_ready, "mv_ready": mv_ready,
                     "rstd_ready": rstd_ready, "biased": biased, "tops_ready": tops_ready,
                     "exps_ready": exps_ready, "tanh_ready": tanh_ready, "stored": stored,
                     "sent_k": sent["k"], "sent_v": sent["v"], "fetched_k": fetched["k"],
                     "fetched_v": fetched["v"], "multiplied": multiplied, "reduced": reduced,
                     "centred": centred, "weighted": weighted, "window_exps": window_exps, "ones_ready": ones_ready}

        def group(it, ahead):
            return slice(it + ahead, it + ahead + 1) if isinstance(it, int) else bass.ds(it + ahead, 1)

        with nc.Block() as block:
            @block.sync
            def _(sp):
                for name in WEIGHTS:
                    sp.dma_start(W[name][:], t[name].rearrange("(k p) n -> p k n", p=P)).then_inc(setup_dma, 16)
                for dst, name in ((w_up, "up"), (w_down, "down"), (w_gate, "gate")):
                    sp.dma_start(dst[:], t[name].rearrange("(k p) n -> p k n", p=P)).then_inc(setup_dma, 16)
                for dst, name in ((scale1, "n1"), (scale2, "n2")):
                    sp.dma_start(dst[:], t[name]).then_inc(setup_dma, 16)
                for (l, w), dst in bias_qk.items():
                    sp.dma_start(dst[:], t[f"{NAMES[l]}_b{w}"]).then_inc(setup_dma, 16)
                for (l, w), dst in bias_row.items():
                    src = t[f"{NAMES[l]}_b{w}"].rearrange("(a n) -> a n", a=1).broadcast_to([P, D])
                    sp.dma_start(dst[:], src).then_inc(setup_dma, 16)
                sp.wait_ge(setup_dve, 1)
                for dst in passed.values():
                    for first in (0, T + HALO):
                        sp.dma_start(dst[first:first + HALO], xn[0][0:HALO, 0, :]).then_inc(setup_zeros, 16)
                sp.wait_ge(setup_zeros, 16 * 2 * len(passed))

            @block.gpsimd
            def _(pool):
                nc.gpsimd.memset(ident[:], 0.0).then_inc(setup_pool, 1)
                nc.gpsimd.memset(ident_b[:], 0.0).then_inc(setup_pool, 1)
                nc.gpsimd.memset(causal_mask[:], 0.0).then_inc(setup_pool, 1)
                nc.gpsimd.memset(causal_mask_t[:], 0.0).then_inc(setup_pool, 1)
                nc.gpsimd.memset(edge_mask[:], 0.0).then_inc(setup_pool, 1)
                pool.wait_ge(setup_pool, 5)
                for dst in (ident, ident_b):
                    nc.gpsimd.affine_select(out=dst[:], in_=dst[:], compare_op=ALU.not_equal, fill=1.0, base=0,
                                            pattern=[[-1, P]], channel_multiplier=1).then_inc(setup_pool, 1)
                nc.gpsimd.affine_select(out=causal_mask[:], in_=causal_mask[:], compare_op=ALU.is_ge, fill=NEG,
                                        base=0, pattern=[[0, 4], [-1, P]], channel_multiplier=1).then_inc(setup_pool, 1)
                nc.gpsimd.affine_select(out=causal_mask_t[:], in_=causal_mask_t[:], compare_op=ALU.is_ge, fill=NEG,
                                        base=0, pattern=[[0, 2], [1, P]], channel_multiplier=-1).then_inc(setup_pool, 1)
                nc.gpsimd.affine_select(out=edge_mask[:], in_=edge_mask[:], compare_op=ALU.is_ge, fill=NEG,
                                        base=-HALO, pattern=[[1, 2], [1, WINDOW]],
                                        channel_multiplier=2).then_inc(setup_pool, 1)
                pool.wait_ge(setup_pool, 10)
                nc.gpsimd.affine_select(out=edge_mask[:], in_=edge_mask[:], compare_op=ALU.is_ge, fill=NEG,
                                        base=T - 1 + HALO, pattern=[[-1, 2], [-1, WINDOW]],
                                        channel_multiplier=-2).then_inc(setup_pool, 1)

            @block.vector
            def _(dve):
                nc.vector.memset(xn[0][0:HALO, 0, :], 0.0).then_inc(setup_dve, 1)
                nc.vector.memset(neg_half[:], -0.5)
                for s in range(STREAMS):
                    nc.vector.memset(va[s][:, :, H * VW:VPAD], 0.0)
                    nc.vector.memset(va_heads[s][:, :, :, HD:VW], 1.0)
                dve.wait_ge(setup_dma, 16 * (len(WEIGHTS) + 5 + len(bias_qk) + len(bias_row)))
                for k in range(2):
                    for name in ("causal_q", "causal_k", "causal_v"):
                        nc.vector.tensor_scalar(W[name][:, k], W[name][:, k], scale1[:, k:k + 1], None, ALU.mult)
                    for w in (w_up, w_gate):
                        nc.vector.tensor_scalar(w[:, k], w[:, k], scale2[:, k:k + 1], None, ALU.mult)
                nc.vector.tensor_scalar(w_down[:], w_down[:], 0.5, None, ALU.mult).then_inc(setup_dve, 1)
                dve.wait_ge(setup_dve, 2)

        def body(plan, it):
            order, fills = plan.order, plan.fills

            def wait_taken(eng, at, name, s, *args):
                if plan.earlier(at, (name, s, args)):
                    b, n = fills[name, s, args]
                    eng.wait_ge(emptied[b], n + 1)

            def reached(at, signal, name, s, *args):
                return plan.reached[signal, name, s, args] if plan.earlier(at, (name, s, args)) else 0

            def part_of(w, s, L, part, n):
                v = parts[w][plan.part_slot[s, L]][:, part if w == "q" else 2 - part, 0:2 * n]
                return v.rearrange("p (k t) -> p k t", t=n)

            def chunk_of(s, c):
                half = parts["qk"[c % 2]][plan.part_slot[s, LOCAL]]
                return half.rearrange("p n t -> p (n t)").bitcast(F32)[:, 0:chunk_values(c)]

            def prob_of(s, L, g, kb):
                blocks = key_blocks(L, T, C)
                first, n = sum(4 * b[3] for b in blocks[:kb]), blocks[kb][3]
                return prob[plan.prob_slot[s, L, g]][:, first:first + 4 * n].rearrange("p (h q) -> p h q", q=n)

            with nc.Block(no_gpsimd_drain=True) as block:
                @block.sync
                def _(sp):
                    for at, (name, s, args) in enumerate(order):
                        if name == "load":
                            if count := reached(at, "stored", "store", s):
                                sp.wait_ge(stored[s], count)
                            src = t["x"].rearrange("(n s) (b p) d -> n s p b d", s=STREAMS, p=P)[group(it, 1), s]
                            sp.dma_start(x[s][:], src.rearrange("a p b d -> (a p) b d")).then_inc(x_loaded[s], 16)
                            src = t["ctx_1024"].rearrange("(n s) c d -> n s c d", s=STREAMS)[group(it, 1), s]
                            sp.dma_start(cx[s][0:C, :], src.rearrange("a c d -> (a c) d")).then_inc(ctx_loaded[s], 16)
                        elif name == "send":
                            w, = args
                            wait_taken(sp, at, "project_rows", s, w)
                            dst = passed[s, w][HALO:HALO + T].rearrange("(p b) d -> p (b d)", b=2)
                            sp.dma_start(dst, token_rows[w][s].rearrange("p b d -> p (b d)")).then_inc(sent[w][s], 16)
                        elif name == "fetch":
                            w, = args
                            if count := reached(at, f"sent_{w}", "send", s, w):
                                sp.wait_ge(sent[w][s], count)
                            src = passed[s, w]
                            sp.dma_start(window(w, s, 0, (1, HELD * D)),
                                         bass.AP(src.tensor, src.offset, [[2 * D, P], [1, HELD * D]])).then_inc(
                                             fetched[w][s], 16)
                        elif name == "split":
                            L, w = args
                            keys = C if L == CROSS and w == "k" else T
                            if count := reached(at, f"lo_ready_{w}", "split", s, L, w):
                                sp.wait_ge(lo_ready[w][s], count)
                            src = parts[w][plan.part_slot[s, L]][:, :, 0:2 * keys]
                            dst = spill[s, w][:, :, :, 0:2 * keys].rearrange("n i h x -> (i h) n x")
                            sp.dma_start(dst, src).then_inc(spilled[w][s], 16)
                        elif name == "gather":
                            L, = args
                            for w in "qk":
                                keys = C if L == CROSS and w == "k" else T
                                if count := reached(at, f"spilled_{w}", "split", s, L, w):
                                    sp.wait_ge(spilled[w][s], count)
                                for first, n in RUNS:
                                    part = 0 if w == "q" else 3 - n
                                    src = spill[s, w][part:part + n, :, :, 0:2 * keys].rearrange("n i h x -> (n i) h x")
                                    dst = stack[w][s][HD * first:HD * (first + n), 0:H * keys]
                                    sp.dma_start(dst.rearrange("p (h x) -> p h x", x=2 * keys),
                                                 src).then_inc(stacked[s], 16)
                        elif name == "shift_in":
                            L, = args
                            wait_taken(sp, at, "shift", s, L)
                            for part in range(2):
                                sp.dma_start(stack_of("q", s, T)[SHIFT + part:SHIFT + part + 1],
                                             nmaxT[s][H * part:H * (part + 1)]).then_inc(shift_ready[s], 16)
                        elif name == "store":
                            wait_taken(sp, at, "down", s)
                            dst = out.rearrange("(n s) (b p) d -> n s p b d", s=STREAMS, p=P)[group(it, 0), s]
                            sp.dma_start(dst.rearrange("a p b d -> (a p) b d"), x[s][:]).then_inc(stored[s], 16)
                    for signal in DMA_SIGNALS:
                        for s in range(STREAMS):
                            if (signal, s) in plan.total:
                                sp.wait_ge(signal_of[signal][s], plan.total[signal, s])

                @block.tensor
                def _(pe):
                    def bank(name, s, args):
                        b, n = fills[(name, s, args)]
                        if n:
                            pe.wait_ge(emptied[b], n)
                        return b

                    for at, (name, s, args) in enumerate(order):
                        if name == "turn":
                            i, = args
                            if count := reached(at, "xn_ready", "norm", s, i):
                                pe.wait_ge(xn_ready[s], count)
                            b = bank(name, s, args)
                            for k in range(2):
                                for tb in range(2):
                                    col = k * T + tb * P
                                    last = nc.tensor.transpose(ps[:, b, col:col + P], xn[s][:, tb, k * P:(k + 1) * P],
                                                               ident[:])
                            last.then_inc(filled[b], 1)
                        elif name == "turn_ctx":
                            if count := reached(at, "ctx_loaded", "load", s):
                                pe.wait_ge(ctx_loaded[s], count)
                            b = bank(name, s, args)
                            for k in range(2):
                                last = nc.tensor.transpose(ps[:, b, k * C:(k + 1) * C], cx[s][0:C, k * P:(k + 1) * P],
                                                           ident[0:C, 0:C])
                            last.then_inc(filled[b], 1)
                        elif name == "project_rows":
                            w, = args
                            wait_taken(pe, at, "turn", s, LOCAL)
                            b = bank(name, s, args)
                            for tb in range(2):
                                for k in range(2):
                                    tokens = xT[s][:, k, :].rearrange("p (t b) -> p b t", b=2)[:, tb, :]
                                    last = nc.tensor.matmul(ps[:, b, tb * D:(tb + 1) * D], tokens,
                                                            W[f"local_{w}"][:, k, :], start=(k == 0), stop=(k == 1))
                            last.then_inc(filled[b], 1)
                        elif name == "project":
                            L, w = args
                            src, n = xT[s], T
                            wait_taken(pe, at, "turn", s, L)
                            if L == CROSS and w != "q":
                                wait_taken(pe, at, "turn_ctx", s)
                                src, n = cT[s], C
                            b = bank(name, s, args)
                            wt = W[f"{NAMES[L]}_{w}"]
                            if w in "qk":
                                for m in range(2):
                                    for k in range(2):
                                        last = nc.tensor.matmul(ps[:, b, m * n:(m + 1) * n], wt[:, k, m * P:(m + 1) * P],
                                                                src[:, k, 0:n], start=(k == 0), stop=(k == 1))
                            else:
                                for tb in range((n + P - 1) // P):
                                    rows = min(P, n - tb * P)
                                    for k in range(2):
                                        last = nc.tensor.matmul(ps[0:rows, b, tb * D:(tb + 1) * D],
                                                                src[:, k, tb * P:tb * P + rows], wt[:, k, :],
                                                                start=(k == 0), stop=(k == 1))
                            last.then_inc(filled[b], 1)
                        elif name == "max":
                            L, f = args
                            tb, h0, hs, key0, keys = max_fills(L, T, C)[f]
                            if f == 0:
                                if count := reached(at, "stacked", "gather", s, L):
                                    pe.wait_ge(stacked[s], count)
                            b = bank(name, s, args)
                            to = ps[:, b, 0:hs * keys].rearrange("p (h k) -> p h k", k=keys)
                            qst, kst = stack_of("q", s, T), stack_of("k", s, C if L == CROSS else T)
                            for j in range(hs):
                                last = nc.tensor.matmul(to[:, j, :],
                                                        qst[0:SHIFT, h0 + j, tb * P:(tb + 1) * P],
                                                        kst[0:SHIFT, h0 + j, key0:key0 + keys],
                                                        start=(j == 0), stop=(j == hs - 1), skip_group_check=True)
                            if L == CAUSAL:
                                last = nc.tensor.matmul(to[:, :, tb * P:(tb + 1) * P], ident_b[:],
                                                        causal_mask[:, 0:hs, :], start=False, stop=True,
                                                        skip_group_check=True)
                            last.then_inc(filled[b], 1)
                        elif name == "shift":
                            L, = args
                            if count := reached(at, "nmax_ready", "round_max", s, L):
                                pe.wait_ge(nmax_ready[s], count)
                            b = bank(name, s, args)
                            to = ps[:, b, :].bitcast(BF16)
                            for tb in range(2):
                                last = nc.tensor.transpose(to[0:2 * H, tb * P:(tb + 1) * P], nmax_parts[s][:, tb, :],
                                                           ident_b[:])
                            last.then_inc(filled[b], 1)
                        elif name == "scores":
                            L, g, kb = args
                            key0, keys, q0, qs = key_blocks(L, T, C)[kb]
                            if g == 0 and kb == 0:
                                if count := reached(at, "shift_ready", "shift_in", s, L):
                                    pe.wait_ge(shift_ready[s], count)
                                if count := reached(at, "ones_ready", "ones", s):
                                    pe.wait_ge(ones_ready[s], count)
                            b = bank(name, s, args)
                            first = SINGLES + 2 * (b - SINGLES)
                            qst, kst = stack_of("q", s, T), stack_of("k", s, C if L == CROSS else T)
                            for half in range(2):
                                to = ps[0:keys, first + half, 0:2 * qs].rearrange("p (h q) -> p h q", q=qs)
                                for j in range(2):
                                    head = 4 * g + 2 * half + j
                                    last = nc.tensor.matmul(to[:, j, :],
                                                            kst[0:STACK, head, key0:key0 + keys],
                                                            qst[0:STACK, head, q0:q0 + qs],
                                                            start=(j == 0), stop=(j == 1), skip_group_check=True)
                                if L == CAUSAL:
                                    last = nc.tensor.matmul(to[:, :, 0:P], ident_b[:], causal_mask_t[:, 0:2, :],
                                                            start=False, stop=True, skip_group_check=True)
                            last.then_inc(filled[b], 1)
                        elif name == "values":
                            L, g = args
                            blocks = key_blocks(L, T, C)
                            nkb = len(blocks)
                            wait_taken(pe, at, "project", s, L, "v")
                            for kb in range(nkb):
                                wait_taken(pe, at, "scores", s, L, g, kb)
                            b = bank(name, s, args)
                            for kb, (key0, keys, q0, qs) in enumerate(blocks):
                                pr = prob_of(s, L, g, kb)
                                for j in range(4):
                                    last = nc.tensor.matmul(ps[SLOT * j:SLOT * (j + 1), b, q0:q0 + qs],
                                                            va[s][0:keys, kb, VW * (4 * g + j):VW * (4 * g + j) + SLOT],
                                                            pr[0:keys, j, :],
                                                            start=(kb == 0), stop=(kb == nkb - 1),
                                                            tile_position=(0, SLOT * j), skip_group_check=True)
                            last.then_inc(filled[b], 1)
                        elif name == "untangle":
                            L, tb = args
                            wait_taken(pe, at, "values", s, L, 3)
                            b = bank(name, s, args)
                            for g in range(4):
                                last = nc.tensor.transpose(ps[:, b, g * P:(g + 1) * P],
                                                           acc[s][:, g, tb * P:(tb + 1) * P], ident[:])
                            last.then_inc(filled[b], 1)
                        elif name == "turn_out":
                            L, = args
                            if L != LOCAL:
                                wait_taken(pe, at, "untangle", s, L, 1)
                            elif count := reached(at, "reduced", "window_reduce", s, len(CHUNKS) - 1):
                                pe.wait_ge(reduced[s], count)
                            b = bank(name, s, args)
                            for k in range(2):
                                for tb in range(2):
                                    col = k * T + tb * P
                                    last = nc.tensor.transpose(ps[:, b, col:col + P], o[s][:, tb, k * P:(k + 1) * P],
                                                               ident[:])
                            last.then_inc(filled[b], 1)
                        elif name == "project_out":
                            L, = args
                            wait_taken(pe, at, "turn_out", s, L)
                            b = bank(name, s, args)
                            for tb in range(2):
                                for k in range(2):
                                    last = nc.tensor.matmul(ps[:, b, tb * D:(tb + 1) * D],
                                                            xT[s][:, k, tb * P:(tb + 1) * P],
                                                            W[f"{NAMES[L]}_o"][:, k, :], start=(k == 0), stop=(k == 1))
                            last.then_inc(filled[b], 1)
                        elif name == "gate":
                            wait_taken(pe, at, "turn", s, 3)
                            b = bank(name, s, args)
                            for tb in range(2):
                                for k in range(2):
                                    last = nc.tensor.matmul(ps[:, b, tb * E:(tb + 1) * E],
                                                            xT[s][:, k, tb * P:(tb + 1) * P], w_gate[:, k, :],
                                                            start=(k == 0), stop=(k == 1))
                            last.then_inc(filled[b], 1)
                        elif name == "up":
                            m2, = args
                            wait_taken(pe, at, "turn", s, 3)
                            b = bank(name, s, args)
                            for m in range(2):
                                for k in range(2):
                                    last = nc.tensor.matmul(ps[:, b, m * T:(m + 1) * T],
                                                            w_up[:, k, (2 * m2 + m) * P:(2 * m2 + m + 1) * P],
                                                            xT[s][:, k, :], start=(k == 0), stop=(k == 1))
                            last.then_inc(filled[b], 1)
                        elif name == "down":
                            wait_taken(pe, at, "up", s, 3)
                            b = bank(name, s, args)
                            for tb in range(2):
                                for m in range(F // P):
                                    last = nc.tensor.matmul(ps[:, b, tb * D:(tb + 1) * D],
                                                            hid[s][:, m, tb * P:(tb + 1) * P], w_down[:, m, :],
                                                            start=(m == 0), stop=(m == F // P - 1))
                            last.then_inc(filled[b], 1)

                @block.scalar
                def _(act):
                    def bank(name, s, args):
                        b, n = fills[(name, s, args)]
                        act.wait_ge(filled[b], n + 1)
                        return b

                    steps = [0]

                    def settle(ins):
                        steps[0] += 1
                        ins.then_inc(act_step, 1)
                        act.wait_ge(act_step, steps[0])

                    for at, (name, s, args) in enumerate(order):
                        if name == "norm":
                            i, = args
                            if count := reached(at, "rstd_ready", "moments", s, i):
                                act.wait_ge(rstd_ready[s], count)
                            if i < 3:
                                dst = xn[s] if i < 2 else y[s]
                                for tb in range(2):
                                    last = nc.scalar.activation(dst[:, tb, :], x[s][:, tb, :], ACT.Identity,
                                                                bias=nmean[s][:, tb:tb + 1],
                                                                scale=rstd[s][:, tb:tb + 1])
                                if i == 2:
                                    settle(last)
                            if i >= 2:
                                for tb in range(2):
                                    last = nc.scalar.activation(xn[s][:, tb, :], y[s][:, tb, :], ACT.Identity,
                                                                scale=rrms[s][:, tb:tb + 1])
                            last.then_inc(xn_ready[s], 1)
                        elif name == "turn":
                            b = bank(name, s, args)
                            nc.scalar.copy(xT[s][:].rearrange("p k t -> p (k t)"),
                                           ps[:, b, :]).then_inc(emptied[b], 1)
                        elif name == "turn_ctx":
                            b = bank(name, s, args)
                            nc.scalar.copy(y[s][:, 1, 0:2 * C],
                                           ps[:, b, 0:2 * C]).then_inc(emptied[b], 1)
                        elif name == "project" and args[1] != "v":
                            L, w = args
                            n = C if L == CROSS and w == "k" else T
                            before = plan.part_before[s, L]
                            if before and before[1] == LOCAL:
                                act.wait_ge(reduced[before[0]], plan.reached["reduced", "window_reduce", before[0],
                                                                             (len(CHUNKS) - 1,)])
                            elif before:
                                if count := reached(at, f"spilled_{w}", "split", *before, w):
                                    act.wait_ge(spilled[w][before[0]], count)
                            b = bank(name, s, args)
                            hi = part_of(w, s, L, 0, n)
                            v = ps[:, b, 0:2 * n].rearrange("p (m t) -> p m t", t=n)
                            if L == CAUSAL:
                                last = nc.scalar.copy(hi, v)
                            else:
                                for m in range(2):
                                    last = nc.scalar.activation(hi[:, m, :], v[:, m, :], ACT.Identity,
                                                                bias=bias_qk[L, w][:, m:m + 1])
                            last.then_inc(hi_ready[s], 1)
                        elif name == "split":
                            L, w = args
                            n = C if L == CROSS and w == "k" else T
                            wait_taken(act, at, "project", s, L, w)
                            nc.scalar.copy(part_of(w, s, L, 1, n),
                                           rest[s][:, "qk".index(w), :, 0:n]).then_inc(mid_ready[s], 1)
                        elif name == "scores":
                            L, g, kb = args
                            key0, keys, q0, qs = key_blocks(L, T, C)[kb]
                            b = bank(name, s, args)
                            first = SINGLES + 2 * (b - SINGLES)
                            before = plan.prob_before[s, L, g]
                            if before and kb == 0:
                                b2, n2 = fills["values", before[0], before[1:]]
                                act.wait_ge(filled[b2], n2 + 1)
                            dst = prob_of(s, L, g, kb).rearrange("p (a h) q -> p a (h q)", a=2)
                            nc.scalar.activation(dst[0:keys], ps[0:keys, first:first + 2, 0:2 * qs], ACT.Exp,
                                                 scale=SCALE).then_inc(emptied[b], 1)
                        elif name == "values":
                            L, g = args
                            b = bank(name, s, args)
                            nc.scalar.copy(acc[s][:, g, :],
                                           ps[:, b, 0:T]).then_inc(emptied[b], 1)
                        elif name == "window_exp":
                            if count := reached(at, "centred", "window_max", s):
                                act.wait_ge(centred[s], count)
                            nc.scalar.activation(window_probs[s], window_probs[s], ACT.Exp,
                                                 scale=SCALE).then_inc(window_exps[s], 1)
                        elif name == "turn_out":
                            L, = args
                            b = bank(name, s, args)
                            if L == LOCAL:
                                dst = xT[s][:].rearrange("p k (t b) -> p k b t", b=2)
                                src = ps[:, b, :].rearrange("p (k b t) -> p k b t", k=2, b=2)
                                for k in range(2):
                                    last = nc.scalar.copy(dst[:, k], src[:, k])
                                last.then_inc(emptied[b], 1)
                            else:
                                nc.scalar.copy(xT[s][:].rearrange("p k t -> p (k t)"),
                                               ps[:, b, :]).then_inc(emptied[b], 1)
                        elif name == "gate":
                            if count := reached(at, "tops_ready", "gate", s):
                                act.wait_ge(tops_ready[s], count)
                            for tb in range(2):
                                nc.scalar.activation(expl[s][:, tb, :], logits[s][:, tb, :], ACT.Exp,
                                                     bias=ntop[s][:, tb:tb + 1], accum_out=zsum[s][:, tb:tb + 1])
                                last = nc.scalar.activation(expt[s][:, tb, :], top[s][:, tb, 0:2], ACT.Exp,
                                                            bias=ntop[s][:, tb:tb + 1],
                                                            accum_out=tsum[s][:, tb:tb + 1])
                            last.then_inc(exps_ready[s], 1)
                        elif name == "up":
                            m2, = args
                            b = bank(name, s, args)
                            if m2 >= 2:
                                wait_taken(act, at, "up", s, m2 - 2)
                            nc.scalar.activation(tanh[s][:, m2 % 2].rearrange("p m t -> p (m t)"), ps[:, b, :],
                                                 ACT.Tanh, scale=0.5).then_inc(tanh_ready[s], 1)

                @block.gpsimd
                def _(pool):
                    steps = [0]

                    def settle(ins):
                        steps[0] += 1
                        ins.then_inc(pool_step, 1)
                        pool.wait_ge(pool_step, steps[0])

                    for at, (name, s, args) in enumerate(order):
                        if name == "moments":
                            i, = args
                            if count := reached(at, "mv_ready", "moments", s, i):
                                pool.wait_ge(mv_ready[s], count)
                            mean, var = mv[s][:, :, 0], mv[s][:, :, 1]
                            if i < 3:
                                settle(nc.gpsimd.tensor_scalar(ms[s][:], var, LN_EPS, None, ALU.add))
                                settle(nc.gpsimd.tensor_tensor(rstd[s][:], ms[s][:], neg_half[:], ALU.pow))
                                settle(nc.gpsimd.tensor_tensor(nmean[s][:], mean, rstd[s][:], ALU.mult))
                                last = nc.gpsimd.tensor_scalar(nmean[s][:], nmean[s][:], -1.0, None, ALU.mult)
                            if i == 2:
                                settle(nc.gpsimd.tensor_tensor(ms[s][:], rstd[s][:], rstd[s][:], ALU.mult))
                                settle(nc.gpsimd.tensor_tensor(ms[s][:], ms[s][:], var, ALU.mult))
                            elif i == 3:
                                settle(nc.gpsimd.tensor_tensor(ms[s][:], mean, mean, ALU.mult))
                                settle(nc.gpsimd.tensor_tensor(ms[s][:], ms[s][:], var, ALU.add))
                            if i >= 2:
                                settle(nc.gpsimd.tensor_scalar(ms[s][:], ms[s][:], RMS_EPS, None, ALU.add))
                                last = nc.gpsimd.tensor_tensor(rrms[s][:], ms[s][:], neg_half[:], ALU.pow)
                            last.then_inc(rstd_ready[s], 1)
                        elif name == "norm":
                            i, = args
                            if i < 2:
                                if count := reached(at, "xn_ready", "norm", s, i):
                                    pool.wait_ge(xn_ready[s], count)
                                row = bias_row[i, "o"]
                                for tb in range(2):
                                    last = nc.gpsimd.tensor_tensor(x[s][:, tb, :], x[s][:, tb, :], row[:], ALU.add)
                                last.then_inc(biased[s], 1)
                            elif i == 3:
                                wait_taken(pool, at, "project_out", s, CAUSAL)
                                nc.gpsimd.tensor_tensor(x[s][:], x[s][:], y[s][:], ALU.add).then_inc(biased[s], 1)
                        elif name == "window_times":
                            c, = args
                            w, b, first, n = CHUNKS[c]
                            before = plan.part_before[s, LOCAL]
                            if c < 2 and before and before[1] == LOCAL:
                                pool.wait_ge(reduced[before[0]], plan.reached["reduced", "window_reduce", before[0],
                                                                              (len(CHUNKS) - 1,)])
                            elif c < 2 and before:
                                w2 = "qk"[c]
                                pool.wait_ge(spilled[w2][before[0]],
                                             plan.reached[f"spilled_{w2}", "split", before[0], (before[1], w2)])
                            elif c >= 2 and (count := reached(at, "reduced", "window_reduce", s, c - 2)):
                                pool.wait_ge(reduced[s], count)
                            if c == 0:
                                wait_taken(pool, at, "project_rows", s, "q")
                                if count := reached(at, "fetched_k", "fetch", s, "k"):
                                    pool.wait_ge(fetched["k"][s], count)
                            elif c == DOTS:
                                if count := reached(at, "fetched_v", "fetch", s, "v"):
                                    pool.wait_ge(fetched["v"][s], count)
                                if count := reached(at, "weighted", "window_sum", s):
                                    pool.wait_ge(weighted[s], count)
                            if w == "k":
                                q_row = token_rows["q"][s][:, b, :].unsqueeze(1).to_broadcast([P, n, D])
                                last = nc.gpsimd.tensor_tensor(
                                    chunk_of(s, c).rearrange("p (j d) -> p j d", d=D), q_row,
                                    window("k", s, (b + first) * D, (D, n), (1, D)), ALU.mult)
                            else:
                                p = window_probs[s][:, b, :, first:first + n].rearrange("p j h -> p h j")
                                last = nc.gpsimd.tensor_tensor(
                                    chunk_of(s, c).rearrange("p (h i j) -> p h i j", i=HD, j=WINDOW),
                                    window("v", s, b * D + first * HD, (HD, n), (1, HD), (D, WINDOW)),
                                    p.unsqueeze(2).to_broadcast([P, n, HD, WINDOW]), ALU.mult)
                            last.then_inc(multiplied[s], 1)
                        elif name == "ones":
                            if count := reached(at, "reduced", "window_reduce", s, len(CHUNKS) - 1):
                                pool.wait_ge(reduced[s], count)
                            nc.gpsimd.memset(wide[s][:, H * T // 2:H * T], ONES_PAIR).then_inc(ones_ready[s], 1)
                    for s in range(STREAMS):
                        if ("ones_ready", s) in plan.total:
                            pool.wait_ge(ones_ready[s], plan.total["ones_ready", s])
                        if ("biased", s) in plan.total:
                            pool.wait_ge(biased[s], plan.total["biased", s])

                @block.vector
                def _(dve):
                    steps = [0]

                    def settle(ins):
                        steps[0] += 1
                        ins.then_inc(dve_step, 1)
                        dve.wait_ge(dve_step, steps[0])

                    def bank(name, s, args):
                        b, n = fills[(name, s, args)]
                        dve.wait_ge(filled[b], n + 1)
                        return b

                    for at, (name, s, args) in enumerate(order):
                        if name == "moments":
                            i, = args
                            src = y[s] if i == 3 else x[s]
                            if i == 0:
                                if count := reached(at, "x_loaded", "load", s):
                                    dve.wait_ge(x_loaded[s], count)
                            else:
                                wait_taken(dve, at, "project_out", s, i - 1)
                            for tb in range(2):
                                last = nc.vector.bn_stats(stats[s][:, tb, :], src[:, tb, :])
                            settle(last)
                            for tb in range(2):
                                last = nc.vector.bn_aggr(mv[s][:, tb, :], stats[s][:, tb, :])
                            last.then_inc(mv_ready[s], 1)
                        elif name == "project_rows":
                            w, = args
                            b = bank(name, s, args)
                            row = bias_row[LOCAL, w][:].unsqueeze(1).to_broadcast([P, 2, D])
                            nc.vector.tensor_tensor(token_rows[w][s], ps[:, b, :].rearrange("p (b d) -> p b d", b=2), row,
                                                    ALU.add).then_inc(emptied[b], 1)
                        elif name == "window_reduce":
                            c, = args
                            w, b, first, n = CHUNKS[c]
                            if count := reached(at, "multiplied", "window_times", s, c):
                                dve.wait_ge(multiplied[s], count)
                            if w == "k":
                                to = window_probs[s][:, b, first:first + n, :].rearrange("p j h -> p (j h)")
                                width = HD
                            else:
                                to = o[s][:, b, first * HD:(first + n) * HD]
                                width = WINDOW
                            nc.vector.tensor_reduce(to, chunk_of(s, c).rearrange("p (x i) -> p x i", i=width),
                                                    AX_X, ALU.add).then_inc(reduced[s], 1)
                        elif name == "window_max":
                            if count := reached(at, "reduced", "window_reduce", s, DOTS - 1):
                                dve.wait_ge(reduced[s], count)
                            v = window_probs[s]
                            flat = v.rearrange("p b j h -> p (b j) h")
                            edge = edge_mask[:].rearrange("p b j -> p (b j)")
                            settle(nc.vector.tensor_tensor(
                                flat, flat, edge.unsqueeze(2).to_broadcast([P, 2 * WINDOW, H]), ALU.add))
                            settle(nc.vector.tensor_reduce(nmax[s][:], v.rearrange("p b j h -> p b h j"),
                                                           AX_X, ALU.max))
                            nc.vector.tensor_tensor(v, v, nmax[s][:].unsqueeze(2).to_broadcast([P, 2, WINDOW, H]),
                                                    ALU.subtract).then_inc(centred[s], 1)
                        elif name == "window_sum":
                            if count := reached(at, "window_exps", "window_exp", s):
                                dve.wait_ge(window_exps[s], count)
                            v = window_probs[s]
                            settle(nc.vector.tensor_reduce(rsum[s][:], v.rearrange("p b j h -> p b h j"),
                                                           AX_X, ALU.add))
                            settle(nc.vector.reciprocal(rsum[s][:], rsum[s][:]))
                            nc.vector.tensor_tensor(v, v, rsum[s][:].unsqueeze(2).to_broadcast([P, 2, WINDOW, H]),
                                                    ALU.mult).then_inc(weighted[s], 1)
                        elif name == "project":
                            L, w = args
                            b = bank(name, s, args)
                            if w in "qk":
                                n = C if L == CROSS and w == "k" else T
                                hi = part_of(w, s, L, 0, n)
                                r = rest[s][:, "qk".index(w), :, 0:n]
                                v = ps[:, b, 0:2 * n].rearrange("p (m t) -> p m t", t=n)
                                if count := reached(at, "hi_ready", "project", s, L, w):
                                    dve.wait_ge(hi_ready[s], count)
                                if L == CAUSAL:
                                    last = nc.vector.tensor_tensor(r, v, hi, ALU.subtract)
                                else:
                                    for m in range(2):
                                        last = nc.vector.scalar_tensor_tensor(r[:, m, :], v[:, m, :],
                                                                              bias_qk[L, w][:, m:m + 1], hi[:, m, :],
                                                                              ALU.add, ALU.subtract)
                                last.then_inc(emptied[b], 1)
                            else:
                                blocks = 1 if L == CROSS else 2
                                rows = C if L == CROSS else P
                                for tb in range(blocks):
                                    dst = va_heads[s][0:rows, tb, :, 0:HD]
                                    src = ps[0:rows, b, tb * D:(tb + 1) * D].rearrange("p (h i) -> p h i", i=HD)
                                    if L == CAUSAL:
                                        last = nc.vector.tensor_copy(dst, src)
                                    else:
                                        row = bias_row[L, "v"][0:rows, :].rearrange("p (h i) -> p h i", i=HD)
                                        last = nc.vector.tensor_tensor(dst, src, row, ALU.add)
                                last.then_inc(emptied[b], 1)
                        elif name == "split":
                            L, w = args
                            n = C if L == CROSS and w == "k" else T
                            if count := reached(at, "mid_ready", "split", s, L, w):
                                dve.wait_ge(mid_ready[s], count)
                            nc.vector.tensor_tensor(part_of(w, s, L, 2, n), rest[s][:, "qk".index(w), :, 0:n],
                                                    part_of(w, s, L, 1, n),
                                                    ALU.subtract).then_inc(lo_ready[w][s], 1)
                        elif name == "max":
                            L, f = args
                            tb, h0, hs, key0, keys = max_fills(L, T, C)[f]
                            b = bank(name, s, args)
                            nc.vector.tensor_reduce(nmax[s][:, tb, h0:h0 + hs],
                                                    ps[:, b, 0:hs * keys].rearrange("p (h k) -> p h k", k=keys),
                                                    AX_X, ALU.max, negate=True).then_inc(emptied[b], 1)
                        elif name == "round_max":
                            L, = args
                            wait_taken(dve, at, "max", s, L, len(max_fills(L, T, C)) - 1)
                            hi, lo = nmax_parts[s][:, :, 0:H], nmax_parts[s][:, :, H:2 * H]
                            settle(nc.vector.tensor_copy(hi, nmax[s][:]))
                            settle(nc.vector.tensor_tensor(nmax_rest[s][:], nmax[s][:], hi, ALU.subtract))
                            nc.vector.tensor_copy(lo, nmax_rest[s][:]).then_inc(nmax_ready[s], 1)
                        elif name == "shift":
                            b = bank(name, s, args)
                            nc.vector.tensor_copy(nmaxT[s][0:2 * H, :],
                                                  ps[:, b, :].bitcast(BF16)[0:2 * H, 0:T]).then_inc(emptied[b], 1)
                        elif name == "untangle":
                            L, tb = args
                            b = bank(name, s, args)
                            v = ps[:, b, :].rearrange("p (h i) -> p h i", i=SLOT)
                            settle(nc.vector.reciprocal(rsum[s][:, tb, :], v[:, :, HD]))
                            nc.vector.tensor_tensor(o[s][:, tb, :].rearrange("p (h i) -> p h i", i=HD), v[:, :, 0:HD],
                                                    rsum[s][:, tb, :].unsqueeze(2).to_broadcast([P, H, HD]),
                                                    ALU.mult).then_inc(emptied[b], 1)
                        elif name == "project_out":
                            L, = args
                            b = bank(name, s, args)
                            dst = x[s] if L < 2 else y[s]
                            if L < 2:
                                if count := reached(at, "biased", "norm", s, L):
                                    dve.wait_ge(biased[s], count)
                            v = dst[:].rearrange("p b d -> p (b d)")
                            nc.vector.tensor_tensor(v, v, ps[:, b, :], ALU.add).then_inc(emptied[b], 1)
                        elif name == "gate":
                            b = bank(name, s, args)
                            lg = logits[s]
                            nc.vector.tensor_copy(lg[:].rearrange("p b e -> p (b e)"),
                                                  ps[:, b, 0:2 * E]).then_inc(emptied[b], 1)
                            wait_taken(dve, at, "gate", s)
                            for tb in range(2):
                                last = nc.vector.max(top[s][:, tb, :], lg[:, tb, :])
                            settle(last)
                            nc.vector.tensor_scalar(ntop[s][:], top[s][:, :, 0], -1.0, None,
                                                    ALU.mult).then_inc(tops_ready[s], 1)
                        elif name == "up":
                            m2, = args
                            b = bank(name, s, args)
                            if count := reached(at, "tanh_ready", "up", s, m2):
                                dve.wait_ge(tanh_ready[s], count)
                            nc.vector.scalar_tensor_tensor(
                                hid[s][:, 2 * m2:2 * m2 + 2, :].rearrange("p m t -> p (m t)"),
                                tanh[s][:, m2 % 2].rearrange("p m t -> p (m t)"), 1.0, ps[:, b, :],
                                ALU.add, ALU.mult).then_inc(emptied[b], 1)
                        elif name == "weigh":
                            if count := reached(at, "exps_ready", "gate", s):
                                dve.wait_ge(exps_ready[s], count)
                            settle(nc.vector.reciprocal(fac_r[s][:], zsum[s][:]))
                            settle(nc.vector.tensor_tensor(fac[s][:], tsum[s][:], fac_r[s][:], ALU.mult))
                            settle(nc.vector.tensor_scalar(zsum[s][:], fac[s][:], 1e-9, None, ALU.add))
                            settle(nc.vector.reciprocal(fac_r[s][:], zsum[s][:]))
                            settle(nc.vector.tensor_tensor(fac[s][:], fac[s][:], fac_r[s][:], ALU.mult))
                        elif name == "down":
                            b = bank(name, s, args)
                            if count := reached(at, "biased", "norm", s, 3):
                                dve.wait_ge(biased[s], count)
                            for tb in range(2):
                                last = nc.vector.scalar_tensor_tensor(x[s][:, tb, :], ps[:, b, tb * D:(tb + 1) * D],
                                                                      fac[s][:, tb:tb + 1], x[s][:, tb, :],
                                                                      ALU.mult, ALU.add)
                            last.then_inc(emptied[b], 1)

            nc.all_engine_barrier(sems_to_clear=range(sems[0].num, sems[-1].num + 1))

        body(Plan(T, C, heads=True, tails=False), -1)
        with nc.Fori(0, B // STREAMS - 1) as it:
            body(Plan(T, C, heads=True, tails=True), it)
        body(Plan(T, C, heads=False, tails=True), B // STREAMS - 1)


def kernel(**inputs):
    import concourse.bacc as _bacc
    from concourse.bass_utils import run_bass_kernel_spmd as _run

    a = {k: np.asarray(v) for k, v in inputs.items()}
    D = a["x"].shape[-1]
    lay = {"x": a["x"], "ctx_1024": a["ctx_1024"]}
    for name, layer in (("local", "attn"), ("cross", "xattn")):
        for w in "qkvo":
            lay[f"{name}_{w}"] = a[f"L0_{layer}_W{w}"].T
            lay[f"{name}_b{w}"] = a[f"L0_{layer}_b{w}"]
    for n, w in enumerate("qkv"):
        lay[f"causal_{w}"] = a["L0_ffn_qkv_w"][n * D:(n + 1) * D].T
    lay["causal_o"] = a["L0_ffn_o_w"].T
    H = D // HD
    for name in ("cross", "causal"):
        for w in "qk":
            v = lay[f"{name}_{w}"].reshape(D, H // 2, 2, HD)
            lay[f"{name}_{w}"] = v.transpose(0, 2, 3, 1).reshape(D, D)
    for name in ("cross_bq", "cross_bk"):
        lay[name] = lay[name].reshape(H // 2, 2, HD).transpose(1, 2, 0).reshape(2, P).T
    lay["up"], lay["down"], lay["gate"] = (a[f"L0_ffn_{w}_w"].T for w in ("up", "down", "gate"))
    lay["n1"], lay["n2"] = a["L0_ffn_n1_w"], a["L0_ffn_n2_w"]
    for name in ("n1", "n2"):
        lay[name] = lay[name].reshape(2, P).T

    nc = _bacc.Bacc("TRN2", target_bir_lowering=False, num_devices=1)
    arrays, t = {}, {}
    for name, v in lay.items():
        arrays[f"in_{name}"] = np.ascontiguousarray(v)
        t[name] = nc.dram_tensor(f"in_{name}", v.shape, mybir.dt.from_np(v.dtype), kind="ExternalInput").ap()
    out = nc.dram_tensor("out", a["x"].shape, F32, kind="ExternalOutput").ap()
    decoder(nc, t, out)
    r = _run(nc, [arrays], core_ids=[0])
    return r.results[0]["out"]
```
